# Optimizing a Trainium2 kernel written in Bass

```python
import numpy as np
import jax
import jax.numpy as jnp

def _softmax(x, axis=-1):
    return jax.nn.softmax(x, axis=axis)

def _gelu(x):
    return jax.nn.gelu(x, approximate=True)

def _silu(x):
    return jax.nn.silu(x)

def _sigmoid(x):
    return jax.nn.sigmoid(x)

def _layernorm(x, axis=-1, eps=1e-05):
    m = jnp.mean(x, axis=axis, keepdims=True)
    v = jnp.var(x, axis=axis, keepdims=True)
    return (x - m) / jnp.sqrt(v + eps)

def _scatter_add(tgt, idx, src, axis=0):
    return tgt.at[idx].add(src)

def _segment_sum(src, seg, n):
    return jax.ops.segment_sum(src, seg, n)
kernel_name = 'mk_gps_d1_gnn_r8_623967'

def setup_inputs(seed: int=0):
    np.random.seed(seed)
    _w = jnp.asarray

    def _rec_inputs():
        import jax
        import jax.numpy as jnp
        _gk = jax.random.key(seed)
        x = -0.0003713 + 1 * jax.random.normal(jax.random.fold_in(_gk, 1), (6250, 256), jnp.float32)
        src = jax.random.randint(jax.random.fold_in(_gk, 2), (100000,), 0, 6250, jnp.int32)
        dst = jax.random.randint(jax.random.fold_in(_gk, 3), (100000,), 0, 6250, jnp.int32)
        _o = jnp.argsort(dst, stable=True)
        src = src[_o]
        dst = dst[_o]
        edge_attr_64 = 0.000189758 + 1.00013 * jax.random.normal(jax.random.fold_in(_gk, 11), (100000, 64), jnp.float32)
        return (x, src, dst, edge_attr_64)
    x, src, dst, edge_attr_64 = _rec_inputs()

    def _L0_gnn_setup():
        import jax, jax.numpy as jnp
        import numpy as np
        N = 6250
        E = 100000
        IN_DIM = 256
        HID = 256
        EDGE_DIM = 64
        LN_EPS = 1e-05
        GINE_EPS = 0.0
        key = jax.random.key(seed)
        ks = jax.random.split(key, 12)
        s = lambda fan_in: 1.0 / np.sqrt(fan_in)
        return {'x': jax.random.normal(ks[0], (N, IN_DIM), dtype=jnp.float32), 'edge_index': jax.random.randint(ks[1], (2, E), 0, N, dtype=jnp.int64), 'edge_attr': jax.random.normal(ks[2], (E, EDGE_DIM), dtype=jnp.float32), 'We': jax.random.uniform(ks[3], (EDGE_DIM, IN_DIM), jnp.float32, -s(EDGE_DIM), s(EDGE_DIM)), 'be': jax.random.uniform(ks[4], (IN_DIM,), jnp.float32, -s(EDGE_DIM), s(EDGE_DIM)), 'W1': jax.random.uniform(ks[5], (IN_DIM, HID), jnp.float32, -s(IN_DIM), s(IN_DIM)), 'b1': jax.random.uniform(ks[6], (HID,), jnp.float32, -s(IN_DIM), s(IN_DIM)), 'W2': jax.random.uniform(ks[7], (HID, HID), jnp.float32, -s(HID), s(HID)), 'b2': jax.random.uniform(ks[8], (HID,), jnp.float32, -s(HID), s(HID)), 'gamma': jnp.ones((HID,), dtype=jnp.float32), 'beta': jnp.zeros((HID,), dtype=jnp.float32)}
    _L0_gnn_all = _L0_gnn_setup()
    _L0_gnn_in = {k: v for k, v in _L0_gnn_all.items() if k in ('We', 'be', 'W1', 'b1', 'W2', 'b2', 'gamma', 'beta')}
    del _L0_gnn_all

    def _L0_mix_setup():
        import jax, jax.numpy as jnp
        import numpy as np
        B, N, C = (8, 1024, 256)
        H, D, S = (8, 32, 32)
        HID = 4 * C

        def layernorm(x, w, b, eps=1e-05):
            mu = jnp.mean(x, axis=-1, keepdims=True)
            var = jnp.mean(jnp.square(x - mu), axis=-1, keepdims=True)
            return (x - mu) * jax.lax.rsqrt(var + eps) * w + b

        def linear_no_attn(x, Wx, bx, Wq, Wk, Wv, Wo, bo):
            x_mid = x @ Wx.T + bx
            x_mid = x_mid.reshape(x.shape[0], x.shape[1], H, D).transpose(0, 2, 1, 3)
            q = jax.nn.softmax(x_mid @ Wq.T, axis=-1)
            k = jax.nn.softmax(x_mid @ Wk.T, axis=-2)
            v = x_mid @ Wv.T
            kv = jnp.einsum('bhns,bhnd->bhsd', k, v)
            qkv = jnp.einsum('bhns,bhsd->bhnd', q, kv)
            qkv = qkv.transpose(0, 2, 1, 3).reshape(x.shape[0], x.shape[1], H * D)
            return qkv @ Wo.T + bo
        key = jax.random.key(seed)
        ks = jax.random.split(key, 16)
        s = lambda fan: 1.0 / np.sqrt(fan)
        return {'fx': jax.random.normal(ks[0], (B, N, C), jnp.float32), 'ln1_w': jnp.ones((C,), jnp.float32), 'ln1_b': jnp.zeros((C,), jnp.float32), 'Wx': jax.random.uniform(ks[1], (C, C), jnp.float32, -s(C), s(C)), 'bx': jax.random.uniform(ks[2], (C,), jnp.float32, -s(C), s(C)), 'Wq': jax.random.uniform(ks[3], (S, D), jnp.float32, -s(D), s(D)), 'Wk': jax.random.uniform(ks[4], (S, D), jnp.float32, -s(D), s(D)), 'Wv': jax.random.uniform(ks[5], (D, D), jnp.float32, -s(D), s(D)), 'Wo': jax.random.uniform(ks[6], (C, C), jnp.float32, -s(C), s(C)), 'bo': jax.random.uniform(ks[7], (C,), jnp.float32, -s(C), s(C)), 'ln2_w': jnp.ones((C,), jnp.float32), 'ln2_b': jnp.zeros((C,), jnp.float32), 'W1': jax.random.uniform(ks[8], (HID, C), jnp.float32, -s(C), s(C)), 'b1': jax.random.uniform(ks[9], (HID,), jnp.float32, -s(C), s(C)), 'W2': jax.random.uniform(ks[10], (C, HID), jnp.float32, -s(HID), s(HID)), 'b2': jax.random.uniform(ks[11], (C,), jnp.float32, -s(HID), s(HID))}
    _L0_mix_all = _L0_mix_setup()
    _L0_mix_in = {k: v for k, v in _L0_mix_all.items() if k in ('ln1_w', 'ln1_b', 'Wx', 'bx', 'Wq', 'Wk', 'Wv', 'Wo', 'bo', 'ln2_w', 'ln2_b', 'W1', 'b1', 'W2', 'b2')}
    del _L0_mix_all

    def _L0_ffn_setup():
        import jax, jax.numpy as jnp
        import numpy as np
        B, N, D = (16, 512, 256)
        NUM_EXPERTS, TOP_K, HEADS = (4, 2, 4)
        N_EDGES = 131072
        LN_EPS = 1e-05

        def _layernorm(x, g, b):
            mu = x.mean(-1, keepdims=True)
            var = ((x - mu) ** 2).mean(-1, keepdims=True)
            return (x - mu) * jax.lax.rsqrt(var + LN_EPS) * g + b

        def _forward(x, edge_index, W_gat, att_src, att_dst, b_gat, ln_gamma, ln_beta, W1, b1, W2, b2):
            Bc, Nc, Dc = x.shape
            M = Bc * Nc
            x_flat = x.reshape(M, Dc)
            h = (x_flat @ W_gat).reshape(M, HEADS, NUM_EXPERTS)
            loops = jnp.arange(M, dtype=edge_index.dtype)
            src = jnp.concatenate([edge_index[0], loops])
            dst = jnp.concatenate([edge_index[1], loops])
            a_src = (h * att_src).sum(-1)
            a_dst = (h * att_dst).sum(-1)
            e = jax.nn.leaky_relu(a_src[src] + a_dst[dst], negative_slope=0.2)
            e_max = jax.ops.segment_max(e, dst, num_segments=M)
            ee = jnp.exp(e - e_max[dst])
            denom = jax.ops.segment_sum(ee, dst, num_segments=M)
            alpha = ee / (denom[dst] + 1e-16)
            msg = h[src] * alpha[:, :, None]
            agg = jax.ops.segment_sum(msg, dst, num_segments=M).reshape(M, HEADS * NUM_EXPERTS) + b_gat
            scores = _layernorm(agg, ln_gamma, ln_beta).reshape(M, HEADS, NUM_EXPERTS).mean(1)
            scores = scores.reshape(Bc, Nc, NUM_EXPERTS)
            topk_s, topk_i = jax.lax.top_k(scores, TOP_K)
            w = jax.nn.softmax(topk_s, axis=-1)
            out = jnp.zeros_like(x)
            for ei in range(NUM_EXPERTS):
                g = jnp.where(topk_i == ei, w, 0.0).sum(-1)
                hh = jax.nn.gelu(x @ W1[ei] + b1[ei], approximate=False)
                out = out + g[..., None] * (hh @ W2[ei] + b2[ei])
            return out
        key = jax.random.key(seed)
        ks = jax.random.split(key, 8)
        s = 0.05
        return {'x': jax.random.normal(ks[0], (B, N, D), jnp.float32), 'W_gat': jax.random.normal(ks[1], (D, HEADS * NUM_EXPERTS), jnp.float32) * s, 'att_src': jax.random.normal(ks[2], (HEADS, NUM_EXPERTS), jnp.float32) * s, 'att_dst': jax.random.normal(ks[3], (HEADS, NUM_EXPERTS), jnp.float32) * s, 'b_gat': jnp.zeros((HEADS * NUM_EXPERTS,), jnp.float32), 'ln_gamma': jnp.ones((HEADS * NUM_EXPERTS,), jnp.float32), 'ln_beta': jnp.zeros((HEADS * NUM_EXPERTS,), jnp.float32), 'W1': jax.random.normal(ks[4], (NUM_EXPERTS, D, 2 * D), jnp.float32) * s, 'b1': jnp.zeros((NUM_EXPERTS, 2 * D), jnp.float32), 'W2': jax.random.normal(ks[5], (NUM_EXPERTS, 2 * D, D), jnp.float32) * s, 'b2': jnp.zeros((NUM_EXPERTS, D), jnp.float32), 'edge_index': jax.random.randint(ks[6], (2, N_EDGES), 0, B * N, jnp.int32)}
    _L0_ffn_all = _L0_ffn_setup()
    _L0_ffn_in = {k: v for k, v in _L0_ffn_all.items() if k in ('W_gat', 'att_src', 'att_dst', 'b_gat', 'ln_gamma', 'ln_beta', 'W1', 'b1', 'W2', 'b2', 'edge_index')}
    del _L0_ffn_all
    return {'x': x, 'src': src, 'dst': dst, 'edge_attr_64': edge_attr_64, 'L0_gnn_We': _L0_gnn_in['We'], 'L0_gnn_be': _L0_gnn_in['be'], 'L0_gnn_W1': _L0_gnn_in['W1'], 'L0_gnn_b1': _L0_gnn_in['b1'], 'L0_gnn_W2': _L0_gnn_in['W2'], 'L0_gnn_b2': _L0_gnn_in['b2'], 'L0_gnn_gamma': _L0_gnn_in['gamma'], 'L0_gnn_beta': _L0_gnn_in['beta'], 'L0_mix_ln1_w': _L0_mix_in['ln1_w'], 'L0_mix_ln1_b': _L0_mix_in['ln1_b'], 'L0_mix_Wx': _L0_mix_in['Wx'], 'L0_mix_bx': _L0_mix_in['bx'], 'L0_mix_Wq': _L0_mix_in['Wq'], 'L0_mix_Wk': _L0_mix_in['Wk'], 'L0_mix_Wv': _L0_mix_in['Wv'], 'L0_mix_Wo': _L0_mix_in['Wo'], 'L0_mix_bo': _L0_mix_in['bo'], 'L0_mix_ln2_w': _L0_mix_in['ln2_w'], 'L0_mix_ln2_b': _L0_mix_in['ln2_b'], 'L0_mix_W1': _L0_mix_in['W1'], 'L0_mix_b1': _L0_mix_in['b1'], 'L0_mix_W2': _L0_mix_in['W2'], 'L0_mix_b2': _L0_mix_in['b2'], 'L0_ffn_W_gat': _L0_ffn_in['W_gat'], 'L0_ffn_att_src': _L0_ffn_in['att_src'], 'L0_ffn_att_dst': _L0_ffn_in['att_dst'], 'L0_ffn_b_gat': _L0_ffn_in['b_gat'], 'L0_ffn_ln_gamma': _L0_ffn_in['ln_gamma'], 'L0_ffn_ln_beta': _L0_ffn_in['ln_beta'], 'L0_ffn_W1': _L0_ffn_in['W1'], 'L0_ffn_b1': _L0_ffn_in['b1'], 'L0_ffn_W2': _L0_ffn_in['W2'], 'L0_ffn_b2': _L0_ffn_in['b2'], 'L0_ffn_edge_index': _L0_ffn_in['edge_index']}

def reference(x, src, dst, edge_attr_64, L0_gnn_We, L0_gnn_be, L0_gnn_W1, L0_gnn_b1, L0_gnn_W2, L0_gnn_b2, L0_gnn_gamma, L0_gnn_beta, L0_mix_ln1_w, L0_mix_ln1_b, L0_mix_Wx, L0_mix_bx, L0_mix_Wq, L0_mix_Wk, L0_mix_Wv, L0_mix_Wo, L0_mix_bo, L0_mix_ln2_w, L0_mix_ln2_b, L0_mix_W1, L0_mix_b1, L0_mix_W2, L0_mix_b2, L0_ffn_W_gat, L0_ffn_att_src, L0_ffn_att_dst, L0_ffn_b_gat, L0_ffn_ln_gamma, L0_ffn_ln_beta, L0_ffn_W1, L0_ffn_b1, L0_ffn_W2, L0_ffn_b2, L0_ffn_edge_index):
    import jax
    import jax.numpy as jnp

    def _L0_gnn_ref(x, edge_index, edge_attr, We, be, W1, b1, W2, b2, gamma, beta):
        import jax, jax.numpy as jnp
        import numpy as np
        N = 6250
        E = 100000
        IN_DIM = 256
        HID = 256
        EDGE_DIM = 64
        LN_EPS = 1e-05
        GINE_EPS = 0.0
        src = edge_index[0]
        dst = edge_index[1]
        msg = jax.nn.relu(x[src] + edge_attr @ We + be)
        aggr = jax.ops.segment_sum(msg, dst, num_segments=N)
        z = (1.0 + GINE_EPS) * x + aggr
        h = jax.nn.relu(z @ W1 + b1) @ W2 + b2
        h = jax.nn.relu(h) + x
        mu = jnp.mean(h, axis=-1, keepdims=True)
        var = jnp.var(h, axis=-1, keepdims=True)
        return (h - mu) * jax.lax.rsqrt(var + LN_EPS) * gamma + beta

    def _L0_mix_ref(fx, ln1_w, ln1_b, Wx, bx, Wq, Wk, Wv, Wo, bo, ln2_w, ln2_b, W1, b1, W2, b2):
        import jax, jax.numpy as jnp
        import numpy as np
        B, N, C = (8, 1024, 256)
        H, D, S = (8, 32, 32)
        HID = 4 * C

        def layernorm(x, w, b, eps=1e-05):
            mu = jnp.mean(x, axis=-1, keepdims=True)
            var = jnp.mean(jnp.square(x - mu), axis=-1, keepdims=True)
            return (x - mu) * jax.lax.rsqrt(var + eps) * w + b

        def linear_no_attn(x, Wx, bx, Wq, Wk, Wv, Wo, bo):
            x_mid = x @ Wx.T + bx
            x_mid = x_mid.reshape(x.shape[0], x.shape[1], H, D).transpose(0, 2, 1, 3)
            q = jax.nn.softmax(x_mid @ Wq.T, axis=-1)
            k = jax.nn.softmax(x_mid @ Wk.T, axis=-2)
            v = x_mid @ Wv.T
            kv = jnp.einsum('bhns,bhnd->bhsd', k, v)
            qkv = jnp.einsum('bhns,bhsd->bhnd', q, kv)
            qkv = qkv.transpose(0, 2, 1, 3).reshape(x.shape[0], x.shape[1], H * D)
            return qkv @ Wo.T + bo
        h = linear_no_attn(layernorm(fx, ln1_w, ln1_b), Wx, bx, Wq, Wk, Wv, Wo, bo) + fx
        y = layernorm(h, ln2_w, ln2_b)
        y = jax.nn.gelu(y @ W1.T + b1, approximate=False)
        y = y @ W2.T + b2
        return y + h

    def _L0_ffn_ref(x, W_gat, att_src, att_dst, b_gat, ln_gamma, ln_beta, W1, b1, W2, b2, edge_index):
        import jax, jax.numpy as jnp
        import numpy as np
        B, N, D = (16, 512, 256)
        NUM_EXPERTS, TOP_K, HEADS = (4, 2, 4)
        N_EDGES = 131072
        LN_EPS = 1e-05

        def _layernorm(x, g, b):
            mu = x.mean(-1, keepdims=True)
            var = ((x - mu) ** 2).mean(-1, keepdims=True)
            return (x - mu) * jax.lax.rsqrt(var + LN_EPS) * g + b

        def _forward(x, edge_index, W_gat, att_src, att_dst, b_gat, ln_gamma, ln_beta, W1, b1, W2, b2):
            Bc, Nc, Dc = x.shape
            M = Bc * Nc
            x_flat = x.reshape(M, Dc)
            h = (x_flat @ W_gat).reshape(M, HEADS, NUM_EXPERTS)
            loops = jnp.arange(M, dtype=edge_index.dtype)
            src = jnp.concatenate([edge_index[0], loops])
            dst = jnp.concatenate([edge_index[1], loops])
            a_src = (h * att_src).sum(-1)
            a_dst = (h * att_dst).sum(-1)
            e = jax.nn.leaky_relu(a_src[src] + a_dst[dst], negative_slope=0.2)
            e_max = jax.ops.segment_max(e, dst, num_segments=M)
            ee = jnp.exp(e - e_max[dst])
            denom = jax.ops.segment_sum(ee, dst, num_segments=M)
            alpha = ee / (denom[dst] + 1e-16)
            msg = h[src] * alpha[:, :, None]
            agg = jax.ops.segment_sum(msg, dst, num_segments=M).reshape(M, HEADS * NUM_EXPERTS) + b_gat
            scores = _layernorm(agg, ln_gamma, ln_beta).reshape(M, HEADS, NUM_EXPERTS).mean(1)
            scores = scores.reshape(Bc, Nc, NUM_EXPERTS)
            topk_s, topk_i = jax.lax.top_k(scores, TOP_K)
            w = jax.nn.softmax(topk_s, axis=-1)
            out = jnp.zeros_like(x)
            for ei in range(NUM_EXPERTS):
                g = jnp.where(topk_i == ei, w, 0.0).sum(-1)
                hh = jax.nn.gelu(x @ W1[ei] + b1[ei], approximate=False)
                out = out + g[..., None] * (hh @ W2[ei] + b2[ei])
            return out
        return _forward(x, edge_index, W_gat, att_src, att_dst, b_gat, ln_gamma, ln_beta, W1, b1, W2, b2)
    edge_index = jnp.stack([src, dst])
    xn = _layernorm(x, axis=-1)
    x = x + _L0_gnn_ref(xn, edge_index, edge_attr_64, L0_gnn_We, L0_gnn_be, L0_gnn_W1, L0_gnn_b1, L0_gnn_W2, L0_gnn_b2, L0_gnn_gamma, L0_gnn_beta) + _L0_mix_ref(xn[None], L0_mix_ln1_w, L0_mix_ln1_b, L0_mix_Wx, L0_mix_bx, L0_mix_Wq, L0_mix_Wk, L0_mix_Wv, L0_mix_Wo, L0_mix_bo, L0_mix_ln2_w, L0_mix_ln2_b, L0_mix_W1, L0_mix_b1, L0_mix_W2, L0_mix_b2)[0]
    x = x + _L0_ffn_ref(_layernorm(x, axis=-1)[None], L0_ffn_W_gat, L0_ffn_att_src, L0_ffn_att_dst, L0_ffn_b_gat, L0_ffn_ln_gamma, L0_ffn_ln_beta, L0_ffn_W1, L0_ffn_b1, L0_ffn_W2, L0_ffn_b2, L0_ffn_edge_index)[0]
    return x

_drawn_inputs = setup_inputs


def setup_inputs(seed=0):
    import zlib

    import numpy as np

    out = dict(_drawn_inputs(seed))
    spreads = {'L0_gnn_gamma': (1.0, 0.6),
     'L0_gnn_beta': (0.0, 0.8),
     'L0_mix_ln1_w': (1.0, 0.6),
     'L0_mix_ln1_b': (0.0, 0.529),
     'L0_mix_ln2_w': (1.0, 0.6),
     'L0_mix_ln2_b': (0.0, 2.0),
     'L0_ffn_b_gat': (0.0, 0.8),
     'L0_ffn_ln_gamma': (1.0, 0.6),
     'L0_ffn_ln_beta': (0.0, 2.0),
     'L0_ffn_b1': (0.0, 2.0),
     'L0_ffn_b2': (0.0, 2.0)}
    factors = {'L0_gnn_b1': 64.0,
     'L0_gnn_b2': 53.896,
     'L0_mix_Wx': 4.485,
     'L0_mix_bx': 5.703,
     'L0_mix_Wq': 8.0,
     'L0_mix_Wk': 8.0,
     'L0_mix_Wv': 4.26,
     'L0_mix_Wo': 4.02,
     'L0_mix_bo': 25.176,
     'L0_mix_b1': 64.0,
     'L0_mix_b2': 44.88,
     'L0_ffn_att_src': 31.576,
     'L0_ffn_att_dst': 54.24,
     'edge_attr_64': 8.0,
     'L0_gnn_We': 8.0,
     'L0_gnn_be': 8.0,
     'L0_gnn_W1': 4.094,
     'L0_gnn_W2': 3.493,
     'L0_mix_W1': 8.0,
     'L0_mix_W2': 8.0,
     'L0_ffn_W_gat': 6.139,
     'L0_ffn_W1': 6.763,
     'L0_ffn_W2': 5.439}
    for name, (base, spread) in spreads.items():
        noise = np.random.default_rng([zlib.crc32(name.encode()), seed]).standard_normal(out[name].shape)
        drawn = base * np.exp(spread * noise) if base else spread * noise
        out[name] = jnp.asarray(drawn.astype(out[name].dtype))
    for name, factor in factors.items():
        out[name] = (out[name] * factor).astype(out[name].dtype)
    return out
```

```python
from contextlib import ExitStack

import concourse.bass as bass
from concourse import mybir

F32 = mybir.dt.float32
BF16 = mybir.dt.bfloat16
I32 = mybir.dt.int32
ALU = mybir.AluOpType
ACT = mybir.ActivationFunctionType
AX = mybir.AxisListType

P = 128
N = 6250
D = 256
KD = D // P
NT = -(-N // P)
LAST = N - (NT - 1) * P
NP = NT * P
EPS = 1e-5

B = 8
HB = B // 2
E1 = 100000
W1E = 125
S1 = E1 // (W1E * B)
ED = 64
TABLES = 4

E2 = 131072
S2 = E2 // (P * B)
HEADS = 4
NE = 4
HC = HEADS * NE
ROWC = HEADS + HC
SLOTS = 32
NBIN = 8192
MB = 32
S3 = E2 // (P * MB)
HID = 4 * D
EH = 2 * D
PAD = -1e30

SKIP = False
G = 4
NG = NT // G
assert NG * G + 1 == NT


def mm(x, o):
    return x.rearrange("(o n) -> o n", o=o)


class Chain:

    def __init__(self, eng, sem, base=0):
        self.eng, self.sem, self.n = eng, sem, base

    def done(self, ins):
        ins.then_inc(self.sem, 1)
        self.n += 1

    def last(self):
        self.eng.wait_ge(self.sem, self.n)


def semaphores(nc, ctx):
    made = []

    def sem(name):
        made.append(nc.alloc_semaphore(name))
        return made[-1]

    def give_back():
        nc.clear_and_free_semaphores(made)
        nc.all_engine_barrier()

    ctx.callback(give_back)
    return sem


def build(nc, A, out, upto=99):
    with ExitStack() as ctx:
        def dram(name, shape, dt=F32):
            return nc.dram_tensor(name, shape, dt).ap()

        def sb(name, shape, dt=F32):
            return ctx.enter_context(nc.sbuf_tensor(name, shape, dt))

        M = {"skip": SKIP}
        M["xn_dram"] = dram("xn_dram", [NP, D])
        M["agg"] = [dram(f"agg{t}", [N + W1E, D]) for t in range(TABLES)]
        M["order"] = dram("order", [E2, 1], I32)
        M["erow"] = dram("erow", [(E2 + SLOTS) * ROWC, 1])
        M["row_dram"] = dram("row_dram", [NP, ROWC])
        M["eo_dram"] = dram("eo_dram", [NE, NP, D])
        M["x3T_dram"] = dram("x3T_dram", [P, KD, NP])

        M["ident"] = sb("ident", [P, P])
        M["eps"] = sb("eps", [P, 1])
        M["xn"] = sb("xn", [P, NT, D])
        M["stat"] = sb("stat", [P, NT, 2])
        M["src1"] = sb("src1", [W1E, (S1 + 1) * B], I32)
        M["dst1"] = sb("dst1", [W1E, S1 * B])
        M["src2"] = sb("src2", [P, S2 * B], I32)
        M["dst2"] = sb("dst2", [P, S2 * B])
        M["deg"] = sb("deg", [P, NBIN // P])
        M["off"] = sb("off", [P, NBIN // P])
        M["most"] = sb("most", [P, 2])
        M["mosti"] = sb("mosti", [P, 1], I32)
        M["rows"] = sb("rows", [P, NT, ROWC])
        M["adst"] = sb("adst", [P, NT, HEADS])
        M["wq"] = sb("wq", [P, P])
        M["kv"] = sb("kv", [P, KD, P])
        M["xm_dram"] = dram("xm_dram", [P, KD, NP])
        norm_and_indices(nc, A, M)
        if upto < 1:
            return
        if not M.get("skip"):
            gine_edges(nc, A, M)
        if upto < 2:
            return
        sort_gat_edges(nc, A, M)
        if upto < 3:
            return
        mixer_context(nc, A, M)
        if upto < 4:
            return
        nodes(nc, A, M)
        if upto < 5:
            return
        gat_edges_and_experts(nc, A, M)
        if upto < 6:
            return
        attend_and_combine(nc, A, M, out)


def norm_and_indices(nc, A, M):
    ident, eps, xn, stat = M["ident"], M["eps"], M["xn"], M["stat"]
    with ExitStack() as ctx:
        def sb(name, shape, dt=F32):
            return ctx.enter_context(nc.sbuf_tensor(name, shape, dt))

        sem = semaphores(nc, ctx)

        x_sb = sb("x_sb", [P, NT, D])
        bst = sb("bst", [P, NT, 6])
        mv = sb("mv", [P, NT, 2])
        std = sb("std", [P, NT])
        tmp = sb("tmp", [P, NT])
        zero = sb("zero", [W1E, 3 * D])
        nat = {"src1": sb("nsrc1", [S1, B, W1E], I32), "dst1": sb("ndst1", [S1, B, W1E], I32),
               "src2": sb("nsrc2", [S2, B, P], I32), "dst2": sb("ndst2", [S2, B, P], I32)}
        natf = sb("natf", [P, 2, B, P])
        turned = [ctx.enter_context(nc.psum_tensor(f"turned{h}", [P, HB, P], F32)) for h in range(4)]

        s_x = sem("s_x")
        s_tail = sem("s_tail")
        s_idx = [sem(f"s_idx{q}") for q in range(4)]
        s_fill = sem("s_fill")
        s_filled = sem("s_filled")
        s_dve = sem("s_dve")
        s_var = sem("s_var")
        s_std = sem("s_std")
        s_xn = sem("s_xn")
        s_out = sem("s_out")
        s_id = sem("s_id")
        s_nf = sem("s_nf")
        s_tp = sem("s_tp")
        s_tc = sem("s_tc")
        order = ["src1", "dst1", "src2", "dst2"]
        Q = (NT - 1) // 4

        with nc.Block() as block:
            @block.sync
            def _(sp):
                for q in range(4):
                    sp.dma_start(x_sb[:, q * Q:(q + 1) * Q, :],
                                 A["x"][q * Q * P:(q + 1) * Q * P, :].rearrange("(t p) d -> p t d", p=P)).then_inc(s_x, 16)
                sp.wait_ge(s_tail, 1)
                sp.dma_start(x_sb[0:LAST, NT - 1, :], A["x"][(NT - 1) * P:N, :]).then_inc(s_x, 16)
                sp.wait_ge(s_xn, 1)
                sp.dma_start(M["xn_dram"].rearrange("(t p) d -> p t d", p=P), xn[:, :, :]).then_inc(s_out, 16)
                sp.wait_ge(s_out, 16)

            @block.scalar
            def _(act):
                act.dma_start(nat["src1"][:, :, :], A["src"].rearrange("(s b e) -> s b e", b=B, e=W1E)).then_inc(s_idx[0], 16)
                act.dma_start(nat["dst1"][:, :, :], A["dst"].rearrange("(s b e) -> s b e", b=B, e=W1E)).then_inc(s_idx[1], 16)
                act.dma_start(nat["src2"][:, :, :], A["ei"][0].rearrange("(s b e) -> s b e", b=B, e=P)).then_inc(s_idx[2], 16)
                act.dma_start(nat["dst2"][:, :, :], A["ei"][1].rearrange("(s b e) -> s b e", b=B, e=P)).then_inc(s_idx[3], 16)
                act.wait_ge(s_fill, 1)
                for t in range(TABLES):
                    act.dma_start(M["agg"][t].rearrange("(p a r) d -> p a (r d)", p=W1E, r=3),
                                  zero[:, None, :].broadcast_to([W1E, (N + W1E) // W1E // 3, 3 * D])).then_inc(s_filled, 16)
                act.dma_start(M["erow"][E2 * ROWC:, :].rearrange("(k c) o -> k (c o)", c=ROWC), zero[0:SLOTS, 0:ROWC]).then_inc(s_filled, 16)
                act.wait_ge(s_var, 1)
                act.activation(std[:, :], mv[:, :, 1], ACT.Sqrt, bias=eps[:, 0:1]).then_inc(s_std, 1)
                act.wait_ge(s_var, 2)
                act.activation(std[:, :], mv[:, :, 1], ACT.Sqrt, bias=eps[:, 0:1]).then_inc(s_std, 1)
                act.wait_ge(s_filled, 16 * (TABLES + 1))

            @block.gpsimd
            def _(pool):
                nc.gpsimd.memset(ident[:, :], 0.0).then_inc(s_id, 1)
                pool.wait_ge(s_id, 1)
                nc.gpsimd.affine_select(out=ident[:, :], in_=ident[:, :], compare_op=ALU.not_equal, fill=1.0,
                                        base=0, pattern=[[-1, P]], channel_multiplier=1).then_inc(s_id, 1)

            @block.tensor
            def _(pe):
                pe.wait_ge(s_id, 2)
                for q, name in enumerate(order):
                    e, s = nat[name].shape[2], nat[name].shape[0]
                    pe.wait_ge(s_nf, q + 1)
                    if q >= 2:
                        pe.wait_ge(s_tc, 2 * (q - 1))
                    for b in range(B):
                        t = pe.transpose(turned[2 * (q % 2) + b // HB][0:e, b % HB, 0:s], natf[0:s, q % 2, b, 0:e], ident[0:s, 0:s])
                        if b % HB == HB - 1:
                            t.then_inc(s_tp, 1)

            @block.vector
            def _(dve):
                c = Chain(dve, s_dve)

                def moments(of):
                    for t in range(NT):
                        c.done(nc.vector.bn_stats(bst[:, t, :], of[:, t, :]))
                    c.last()
                    for t in range(NT):
                        c.done(nc.vector.bn_aggr(mv[:, t, :], bst[:, t, :]))
                    c.last()

                def newton(r):
                    c.done(nc.vector.tensor_tensor(tmp[:, :], r, r, ALU.mult))
                    c.done(nc.vector.tensor_scalar(mv[:, :, 1], mv[:, :, 1], EPS, -0.5, ALU.add, ALU.mult))
                    c.last()
                    c.done(nc.vector.tensor_tensor(tmp[:, :], tmp[:, :], mv[:, :, 1], ALU.mult))
                    c.last()
                    c.done(nc.vector.scalar_tensor_tensor(r, tmp[:, :], 1.5, r, ALU.add, ALU.mult))
                    c.last()

                nc.vector.memset(x_sb[:, NT - 1, :], 0.0).then_inc(s_tail, 1)
                nc.vector.memset(zero[:, :], 0.0).then_inc(s_fill, 1)
                nc.vector.memset(eps[:, :], EPS)
                nc.vector.memset(M["src1"][:, S1 * B:], 0)
                dve.wait_ge(s_x, 80)
                moments(x_sb)
                nc.vector.memset(std[:, :], 1.0).then_inc(s_var, 1)
                dve.wait_ge(s_std, 1)
                c.done(nc.vector.reciprocal(std[:, :], std[:, :]))
                c.last()
                newton(std[:, :])
                with dve.Fori(0, NT) as t:
                    nc.vector.tensor_scalar(xn[:, t, :], x_sb[:, t, :], mv[:, t, 0:1], std[:, bass.ds(t, 1)],
                                            ALU.subtract, ALU.mult).then_inc(s_dve, 1)
                c.n += NT
                c.last()
                dve.sem_inc(s_xn, 1)
                moments(xn)
                c.done(nc.vector.tensor_copy(stat[:, :, 0], mv[:, :, 0]))
                c.last()
                dve.sem_inc(s_var, 1)
                dve.wait_ge(s_std, 2)
                c.done(nc.vector.reciprocal(stat[:, :, 1], std[:, :]))
                c.last()
                newton(stat[:, :, 1])
                for q, name in enumerate(order):
                    e, s = nat[name].shape[2], nat[name].shape[0]
                    dve.wait_ge(s_idx[q], 16)
                    if q >= 2:
                        dve.wait_ge(s_tp, 2 * (q - 1))
                    if name == "src2":
                        nc.vector.tensor_scalar(natf[0:s, q % 2, :, 0:e], nat[name][:, :, :], float(N - 1), None, ALU.min).then_inc(s_nf, 1)
                    else:
                        nc.vector.tensor_copy(natf[0:s, q % 2, :, 0:e], nat[name][:, :, :]).then_inc(s_nf, 1)
                    dst = M[name][:, 0:s * B].rearrange("e (s b) -> e b s", b=B)
                    for h in range(2):
                        dve.wait_ge(s_tp, 2 * q + h + 1)
                        nc.vector.tensor_copy(dst[:, h * HB:(h + 1) * HB, :], turned[2 * (q % 2) + h][0:e, :, 0:s]).then_inc(s_tc, 1)


def gine_edges(nc, A, M):
    with ExitStack() as ctx:
        def sb(name, shape, dt=F32):
            return ctx.enter_context(nc.sbuf_tensor(name, shape, dt))

        sem = semaphores(nc, ctx)

        ps_t = ctx.enter_context(nc.psum_tensor("ps_t", [ED, 2, 512], F32))
        ps_e = [ctx.enter_context(nc.psum_tensor(f"ps_e{h}", [W1E, HB * D], F32)) for h in range(2)]
        ps_a = ctx.enter_context(nc.psum_tensor("ps_a", [W1E, HB * D], F32))
        we = sb("we", [ED + 1, D])
        before = sb("before", [W1E, W1E])
        spare = sb("spare", [W1E, 1], I32)
        sparef = sb("sparef", [W1E, 1])
        ea = sb("ea", [W1E, 2, B * ED])
        eaT = sb("eaT", [ED + 1, B, W1E])
        row = sb("row", [W1E, 2, B, W1E], I32)
        same = sb("same", [W1E, 2, B, W1E])
        earlier = sb("earlier", [W1E, B, W1E])
        cnt = sb("cnt", [W1E, B])
        dif = sb("dif", [W1E, B])
        gidx = sb("gidx", [W1E, 2, B], I32)
        sidx = sb("sidx", [W1E, 2, B], I32)
        xg = sb("xg", [W1E, 2, B, D])
        msg = sb("msg", [W1E, B, D])
        agg = sb("agg_sb", [W1E, 2, B, D])

        s_w = sem("s_w")
        s_pass = sem("s_pass")
        s_all1 = sem("s_all1")
        s_const = sem("s_const")
        s_ones = sem("s_ones")
        s_ea = [sem(f"s_ea{q}") for q in range(2)]
        s_row = [sem(f"s_row{q}") for q in range(2)]
        s_gi = sem("s_gi")
        s_g = [[sem(f"s_g{q}{h}") for h in range(2)] for q in range(2)]
        s_same = [sem(f"s_same{q}") for q in range(2)]
        s_si = sem("s_si")
        s_dve = sem("s_dve1")
        s_turn = [sem(f"s_turn{q}") for q in range(2)]
        s_eaT = sem("s_eaT")
        s_e = sem("s_e")
        s_sum = sem("s_sum")
        s_msg = sem("s_msg")
        s_am = [sem(f"s_am{q}") for q in range(2)]
        s_agg = sem("s_agg")
        s_tab = [[sem(f"s_tab{q}{t}") for t in range(TABLES)] for q in range(2)]

        with nc.Block() as block:
            @block.sync
            def _(sp):
                sp.dma_start(we[0:ED, :], A["We"]).then_inc(s_w, 16)
                sp.dma_start(we[ED:ED + 1, :], mm(A["be"], 1)).then_inc(s_w, 16)
                with sp.Fori(0, S1 // 2) as i:
                    for q in range(2):
                        base = (i * 2 + q) * (B * W1E)
                        sp.wait_ge(s_same[q], i)
                        sp.dma_start(row[:, q, :, :].rearrange("p b e -> p (b e)"),
                                     A["dst"][bass.ds(base, B * W1E)].partition_broadcast(W1E)).then_inc(s_row[q], 16)
                        sp.wait_ge(s_turn[q], i)
                        sp.dma_start(ea[:, q, :].rearrange("p (b c) -> p b c", b=B),
                                     A["ea"][bass.ds(base, B * W1E), :].rearrange("(b p) c -> p b c", b=B)).then_inc(s_ea[q], 16)

            @block.gpsimd
            def _(pool):
                nc.gpsimd.memset(before[:, :], 1.0).then_inc(s_all1, 1)
                pool.wait_ge(s_all1, 1)
                nc.gpsimd.affine_select(out=before[:, :], in_=before[:, :], compare_op=ALU.is_gt, fill=0.0,
                                        base=0, pattern=[[-1, W1E]], channel_multiplier=1).then_inc(s_const, 1)
                nc.gpsimd.iota(spare[:, :], pattern=[[0, 1]], base=N, channel_multiplier=1).then_inc(s_const, 1)

                def gather(i, q):
                    pool.wait_ge(s_const, 2)
                    pool.wait_ge(s_gi, i * 2 + (q + 1))
                    pool.sem_inc(s_pass, 1)
                    for b in range(B):
                        pool.indirect_dma_start(xg[:, q, b, :], None, M["xn_dram"],
                                                bass.IndirectOffsetOnAxis(ap=gidx[:, q, b:b + 1], axis=0)).then_inc(s_g[q][b // HB], 16)

                def scatter(i, q):
                    pool.wait_ge(s_si, i * 2 + (q + 1))
                    for b in range(B):
                        if b % HB == 0:
                            pool.wait_ge(s_agg, i * 4 + (2 * q + b // HB + 1))
                        t = b % TABLES
                        if b >= TABLES:
                            pool.wait_ge(s_tab[q][t], i * 32 + 16)
                        elif q == 1:
                            pool.wait_ge(s_tab[0][t], i * 32 + 32)
                        else:
                            pool.wait_ge(s_tab[1][t], i * 32)
                        pool.sem_inc(s_pass, 1)
                        pool.indirect_dma_start(M["agg"][t], bass.IndirectOffsetOnAxis(ap=sidx[:, q, b:b + 1], axis=0),
                                                agg[:, q, b, :], None, compute_op=ALU.add).then_inc(s_tab[q][t], 16)

                gather(0, 0)
                with pool.Fori(0, S1 // 2 - 1) as i:
                    gather(i, 1)
                    scatter(i, 0)
                    gather(i + 1, 0)
                    scatter(i, 1)
                last = S1 // 2 - 1
                gather(last, 1)
                scatter(last, 0)
                scatter(last, 1)
                for q in range(2):
                    for t in range(TABLES):
                        pool.wait_ge(s_tab[q][t], 32 * (S1 // 2))

            @block.tensor
            def _(pe):
                pe.wait_ge(s_w, 32)
                pe.wait_ge(s_ones, 1)
                with pe.Fori(0, S1 // 2) as i:
                    for q in range(2):
                        k = 4 * i + 2 * q
                        pe.wait_ge(s_ea[q], i * 16 + 16)
                        pe.wait_ge(s_eaT, k)
                        pe.sem_inc(s_pass, 1)
                        for b in range(B):
                            t = pe.transpose(ps_t[:, b // HB, (b % HB) * W1E:(b % HB + 1) * W1E],
                                             ea[:, q, b * ED:(b + 1) * ED], M["ident"][0:W1E, 0:W1E])
                        t.then_inc(s_turn[q], 1)
                        for h in range(2):
                            pe.wait_ge(s_eaT, k + (h + 1))
                            pe.wait_ge(s_sum, k + h if h == 0 else k)
                            for b in range(HB):
                                t = pe.matmul(ps_e[h][:, b * D:(b + 1) * D], eaT[:, h * HB + b, :], we[:, :], start=True, stop=True)
                            t.then_inc(s_e, 1)
                        pe.wait_ge(s_same[q], i + 1)
                        for h in range(2):
                            pe.wait_ge(s_msg, k + (h + 1))
                            pe.wait_ge(s_agg, k + h)
                            for b in range(HB):
                                t = pe.matmul(ps_a[:, b * D:(b + 1) * D], same[:, q, h * HB + b, :], msg[:, h * HB + b, :], start=True, stop=True)
                            t.then_inc(s_am[q], 1)

            @block.scalar
            def _(act):
                act.wait_ge(s_ones, 1)
                with act.Fori(0, S1 // 2) as i:
                    for q in range(2):
                        k = 4 * i + 2 * q
                        act.wait_ge(s_turn[q], i + 1)
                        act.wait_ge(s_e, k)
                        for h in range(2):
                            nc.scalar.activation(eaT[0:ED, h * HB:(h + 1) * HB, :],
                                                 ps_t[:, h, 0:HB * W1E].rearrange("c (b e) -> c b e", b=HB), ACT.Copy).then_inc(s_eaT, 1)
                        for h in range(2):
                            act.wait_ge(s_sum, k + (h + 1))
                            nc.scalar.activation(msg[:, h * HB:(h + 1) * HB, :], msg[:, h * HB:(h + 1) * HB, :], ACT.Relu).then_inc(s_msg, 1)
                        for h in range(2):
                            act.wait_ge(s_am[q], i * 2 + (h + 1))
                            if h == 0:
                                for t in range(TABLES):
                                    act.wait_ge(s_tab[q][t], i * 32)
                            nc.scalar.activation(agg[:, q, h * HB:(h + 1) * HB, :].rearrange("p b d -> p (b d)"), ps_a[:, :], ACT.Copy).then_inc(s_agg, 1)

            @block.vector
            def _(dve):
                nc.vector.memset(eaT[ED:ED + 1, :, :], 1.0).then_inc(s_ones, 1)
                dve.wait_ge(s_const, 2)
                nc.vector.tensor_copy(sparef[:, :], spare[:, :]).then_inc(s_dve, 1)
                dve.wait_ge(s_dve, 1)

                def stage(i, q):
                    for h in range(2):
                        dve.wait_ge(s_g[q][h], i * 64)
                    nc.vector.tensor_copy(gidx[:, q, :], M["src1"][:, bass.ds((i * 2 + q) * B, B)]).then_inc(s_gi, 1)

                stage(0, 0)
                with dve.Fori(0, S1 // 2) as i:
                    for q in range(2):
                        k = 4 * i + 2 * q
                        j = 8 * i + 4 * q + 1
                        if q == 0:
                            dve.wait_ge(s_sum, k)
                            stage(i, 1)
                        dve.wait_ge(s_row[q], i * 16 + 16)
                        dve.wait_ge(s_am[q], i * 2)
                        dcol = M["dst1"][:, bass.ds((i * 2 + q) * B, B)]
                        nc.vector.tensor_tensor(same[:, q, :, :], row[:, q, :, :],
                                                dcol[:, :, None].broadcast_to([W1E, B, W1E]), ALU.is_equal).then_inc(s_same[q], 1)
                        dve.wait_ge(s_same[q], i + 1)
                        nc.vector.tensor_tensor(earlier[:, :, :], same[:, q, :, :],
                                                before[:, None, :].broadcast_to([W1E, B, W1E]), ALU.mult).then_inc(s_dve, 1)
                        nc.vector.tensor_scalar(dif[:, :], dcol, -1.0, sparef[:, 0:1], ALU.mult, ALU.add).then_inc(s_dve, 1)
                        dve.wait_ge(s_dve, j + 2)
                        nc.vector.tensor_reduce(cnt[:, :], earlier[:, :, :], AX.X, ALU.max).then_inc(s_dve, 1)
                        dve.wait_ge(s_dve, j + 3)
                        nc.vector.tensor_tensor(dif[:, :], dif[:, :], cnt[:, :], ALU.mult).then_inc(s_dve, 1)
                        dve.wait_ge(s_dve, j + 4)
                        for t in range(TABLES):
                            dve.wait_ge(s_tab[q][t], i * 32)
                        nc.vector.tensor_tensor(sidx[:, q, :], dif[:, :], dcol, ALU.add).then_inc(s_si, 1)
                        for h in range(2):
                            dve.wait_ge(s_e, k + (h + 1))
                            dve.wait_ge(s_g[q][h], i * 64 + 64)
                            if q == 0:
                                dve.wait_ge(s_am[1], i * 2)
                            else:
                                dve.wait_ge(s_am[0], i * 2 + 2)
                            nc.vector.tensor_tensor(msg[:, h * HB:(h + 1) * HB, :].rearrange("p b d -> p (b d)"), ps_e[h][:, :],
                                                    xg[:, q, h * HB:(h + 1) * HB, :].rearrange("p b d -> p (b d)"), ALU.add).then_inc(s_sum, 1)
                        if q == 0:
                            dve.wait_ge(s_sum, k + 2)
                            nxt = (i * 2 + 2) * B
                            for h in range(2):
                                dve.wait_ge(s_g[0][h], i * 64 + 64)
                            nc.vector.tensor_copy(gidx[:, 0, :], M["src1"][:, bass.ds(nxt, B)]).then_inc(s_gi, 1)





def sort_gat_edges(nc, A, M):
    NHI = NBIN // P
    with ExitStack() as ctx:
        def sb(name, shape, dt=F32):
            return ctx.enter_context(nc.sbuf_tensor(name, shape, dt))

        sem = semaphores(nc, ctx)

        ps_cnt = ctx.enter_context(nc.psum_tensor("ps_cnt", [P, NHI], F32))
        ps_off = ctx.enter_context(nc.psum_tensor("ps_off", [P, 2, NHI], F32))
        ps_lt = [ctx.enter_context(nc.psum_tensor(f"ps_lt{h}", [P, HB, P], BF16)) for h in range(2)]
        ps_pr = [ctx.enter_context(nc.psum_tensor(f"ps_pr{h}", [P, HB, NHI], F32)) for h in range(2)]
        ii = sb("ii", [P, S2 * B], I32)
        hi = sb("hi", [P, S2 * B])
        lo = sb("lo", [P, S2 * B])
        iof = sb("iof", [P, P])
        iofi = sb("iofi", [P, P], I32)
        before = sb("before2", [P, HB * P])
        lower = sb("lower", [P, P])
        ones = sb("ones", [P, P])
        identb = sb("identb", [P, P], BF16)
        zerob = sb("zerob", [P, P], BF16)
        row = sb("row2", [P, 2, B, P], I32)
        hot_hi = sb("hot_hi", [P, 2, HB, NHI], BF16)
        hot_lo = sb("hot_lo", [P, 2, HB, P], BF16)
        lt = sb("lt", [P, 2, HB, P])
        cnt = sb("cnt2", [P, 2, NHI])
        tot = sb("tot", [P, 2, NHI])
        junk = sb("junk", [P, 2, HB, HB * P], BF16)
        loc = sb("loc", [P, 2, HB])
        sel = sb("sel", [P, 2, HB, NHI])
        prior = sb("prior", [P, 2, HB])
        pos = sb("pos", [P, 2, B], I32)
        val = sb("val", [P, 2, B], I32)

        s_pool = sem("s_pool")
        s_const = sem("s_constb")
        s_row = [sem(f"s_rowb{q}") for q in range(2)]
        s_dve = sem("s_dveb")
        s_hot1 = sem("s_hot1")
        s_acc1 = [sem(f"s_acc1{h}") for h in range(2)]
        s_all = sem("s_all")
        s_off = sem("s_off")
        s_start = sem("s_start")
        s_hot = sem("s_hot")
        s_loc = [sem(f"s_loc{q}") for q in range(2)]
        s_lt = sem("s_lt")
        s_ltc = sem("s_ltc")
        s_pr = sem("s_pr")
        s_acc = [sem(f"s_acc{h}") for h in range(2)]
        s_cnt = sem("s_cnt")
        s_sel = sem("s_sel")
        s_prior = sem("s_prior")
        s_pos = sem("s_pos")
        s_val = sem("s_val")
        s_go = sem("s_gos")
        s_put = [sem(f"s_puts{q}") for q in range(2)]

        with nc.Block() as block:
            @block.sync
            def _(sp):
                with sp.Fori(0, S2 // 2) as i:
                    for q in range(2):
                        sp.wait_ge(s_loc[q], i * (2 * HB))
                        sp.dma_start(row[:, q, :, :].rearrange("p b e -> p (b e)"),
                                     A["ei"][1][bass.ds((i * 2 + q) * (B * P), B * P)].partition_broadcast(P)).then_inc(s_row[q], 16)

            @block.gpsimd
            def _(pool):
                c = Chain(pool, s_pool)
                c.done(nc.gpsimd.memset(before[:, :], 1.0))
                c.done(nc.gpsimd.memset(lower[:, :], 1.0))
                c.done(nc.gpsimd.iota(iofi[:, :], pattern=[[1, P]], base=0, channel_multiplier=0))
                c.last()
                nc.gpsimd.affine_select(out=before[:, (HB - 1) * P:], in_=before[:, (HB - 1) * P:], compare_op=ALU.is_gt, fill=0.0,
                                        base=0, pattern=[[-1, P]], channel_multiplier=1).then_inc(s_const, 1)
                nc.gpsimd.affine_select(out=lower[:, :], in_=lower[:, :], compare_op=ALU.is_gt, fill=0.0,
                                        base=0, pattern=[[1, P]], channel_multiplier=-1).then_inc(s_const, 1)
                pool.wait_ge(s_start, 1)
                nc.gpsimd.partition_all_reduce(M["most"][:, 1:2], M["most"][:, 0:1], P, bass.bass_isa.ReduceOp.max).then_inc(s_pool, 1)

                with pool.Fori(0, S2 // 2) as i:
                    for q in range(2):
                        pool.wait_ge(s_put[q], i * (16 * B))
                        nc.gpsimd.tensor_copy(val[:, q, :], M["src2"][:, bass.ds((i * 2 + q) * B, B)]).then_inc(s_val, 1)
                        pool.wait_ge(s_val, i * 2 + (q + 1))
                        for h in range(2):
                            pool.wait_ge(s_pos, i * 4 + (2 * q + h + 1))
                            pool.sem_inc(s_go, 1)
                            for b in range(h * HB, h * HB + HB):
                                pool.indirect_dma_start(M["order"], bass.IndirectOffsetOnAxis(ap=pos[:, q, b:b + 1], axis=0),
                                                        val[:, q, b:b + 1], None).then_inc(s_put[q], 16)
                for q in range(2):
                    pool.wait_ge(s_put[q], 16 * B * (S2 // 2))

            @block.tensor
            def _(pe):
                pe.wait_ge(s_dve, 6)
                pe.matmul(ps_cnt[:, :], zerob[:, :], zerob[:, 0:NHI], start=True, stop=False, skip_group_check=True)

                def count(h):
                    for b in range(HB):
                        t = pe.matmul(ps_cnt[:, :], hot_lo[:, h, b, :], hot_hi[:, h, b, :], start=False, stop=False, skip_group_check=True)
                    return t

                with pe.Fori(0, S2) as i:
                    for h in range(2):
                        pe.wait_ge(s_hot1, 2 * i + h + 1)
                        count(h).then_inc(s_acc1[h], 1)
                pe.wait_ge(s_all, 1)
                pe.wait_ge(s_const, 2)
                pe.matmul(ps_off[:, 0, :], lower[:, :], M["deg"][:, :], start=True, stop=True)
                pe.matmul(ps_off[:, 1, :], ones[:, :], M["deg"][:, :], start=True, stop=True).then_inc(s_off, 1)
                pe.wait_ge(s_start, 1)
                pe.matmul(ps_cnt[:, :], M["ident"][:, :], M["off"][:, :], start=True, stop=False, skip_group_check=True)

                def turn(i, h):
                    k = 2 * i + h
                    pe.wait_ge(s_hot, k + 1)
                    pe.wait_ge(s_ltc, k - h)
                    for b in range(HB):
                        t = pe.transpose(ps_lt[h][:, b, :], hot_lo[:, h, b, :], identb[:, :])
                    t.then_inc(s_lt, 1)

                def spread(i, h):
                    k = 2 * i + h
                    pe.wait_ge(s_ltc, k + 1)
                    pe.wait_ge(s_cnt, k + 1)
                    pe.wait_ge(s_sel, k - h)
                    for b in range(HB):
                        t = pe.matmul(ps_pr[h][:, b, :], lt[:, h, b, :], cnt[:, h, :], start=True, stop=True)
                    t.then_inc(s_pr, 1)
                    count(h).then_inc(s_acc[h], 1)

                turn(0, 0)
                with pe.Fori(0, S2 - 1) as i:
                    turn(i, 1)
                    spread(i, 0)
                    turn(i + 1, 0)
                    spread(i, 1)
                turn(S2 - 1, 1)
                spread(S2 - 1, 0)
                spread(S2 - 1, 1)

            @block.scalar
            def _(act):
                for h in range(2):
                    act.wait_ge(s_acc1[h], S2)
                nc.scalar.activation(M["deg"][:, :], ps_cnt[:, :], ACT.Copy).then_inc(s_all, 1)
                act.wait_ge(s_start, 2)
                act.sem_inc(s_cnt, 1)

                def turned(i, h):
                    k = 2 * i + h
                    act.wait_ge(s_lt, k + 1)
                    act.wait_ge(s_pr, k - h)
                    nc.scalar.activation(lt[:, h, :, :], ps_lt[h][:, :, :], ACT.Copy).then_inc(s_ltc, 1)

                def counted(i, h):
                    act.wait_ge(s_acc[h], i + 1)
                    nc.scalar.activation(cnt[:, 1 - h, :], ps_cnt[:, :], ACT.Copy).then_inc(s_cnt, 1)

                turned(0, 0)
                with act.Fori(0, S2 - 1) as i:
                    turned(i, 1)
                    counted(i, 0)
                    turned(i + 1, 0)
                    counted(i, 1)
                turned(S2 - 1, 1)
                counted(S2 - 1, 0)

            @block.vector
            def _(dve):
                c = Chain(dve, s_dve)
                c.done(nc.vector.memset(zerob[:, :], 0.0))
                c.done(nc.vector.memset(ones[:, :], 1.0))
                c.done(nc.vector.tensor_copy(identb[:, :], M["ident"][:, :]))
                c.done(nc.vector.tensor_copy(ii[:, :], M["dst2"][:, :]))
                c.last()
                c.done(nc.vector.tensor_single_scalar(ii[:, :], ii[:, :], 7, ALU.logical_shift_right))
                c.last()
                c.done(nc.vector.tensor_copy(hi[:, :], ii[:, :]))
                c.last()
                c.done(nc.vector.scalar_tensor_tensor(lo[:, :], hi[:, :], -float(P), M["dst2"][:, :], ALU.mult, ALU.add))
                dve.wait_ge(s_pool, 3)
                c.done(nc.vector.tensor_copy(iof[:, :], iofi[:, :]))
                c.last()

                def hot(h, cols, signal):
                    nc.vector.tensor_tensor(hot_hi[:, h, :, :], iof[:, None, 0:NHI].broadcast_to([P, HB, NHI]),
                                            hi[:, cols][:, :, None].broadcast_to([P, HB, NHI]), ALU.is_equal).then_inc(s_dve, 1)
                    nc.vector.tensor_tensor(hot_lo[:, h, :, :], iof[:, None, :].broadcast_to([P, HB, P]),
                                            lo[:, cols][:, :, None].broadcast_to([P, HB, P]), ALU.is_equal).then_inc(signal, 1)

                with dve.Fori(0, S2) as i:
                    for h in range(2):
                        dve.wait_ge(s_acc1[h], i)
                        hot(h, bass.ds(i * B + h * HB, HB), s_hot1)
                c.n += 2 * S2
                dve.wait_ge(s_off, 1)
                c.done(nc.vector.memset(tot[:, :, :], 0.0))
                c.last()
                c.done(nc.vector.tensor_copy(tot[:, 0, 1:NHI], ps_off[:, 1, 0:NHI - 1]))
                c.last()
                w, u = 1, 0
                while w < NHI:
                    c.done(nc.vector.tensor_copy(tot[:, 1 - u, 0:w], tot[:, u, 0:w]))
                    c.done(nc.vector.tensor_tensor(tot[:, 1 - u, w:NHI], tot[:, u, w:NHI], tot[:, u, 0:NHI - w], ALU.add))
                    c.last()
                    w, u = 2 * w, 1 - u
                c.done(nc.vector.tensor_tensor(M["off"][:, :], ps_off[:, 0, :], tot[:, u, :], ALU.add))
                c.done(nc.vector.tensor_reduce(M["most"][:, 0:1], M["deg"][:, 0:NT], AX.X, ALU.max))
                c.last()
                dve.sem_inc(s_start, 1)
                nc.vector.tensor_copy(cnt[:, 0, :], M["off"][:, :]).then_inc(s_start, 1)
                dve.wait_ge(s_pool, 4)
                c.done(nc.vector.tensor_copy(M["mosti"][:, :], M["most"][:, 1:2]))
                c.last()
                base = c.n

                def build(i, q, h, first=None):
                    dve.wait_ge(s_acc[h], 2 * i + q)
                    hot(h, bass.ds(i * (2 * B) + (q * B + h * HB), HB), s_hot)
                    if h == 0:
                        dve.wait_ge(s_row[q], i * 16 + 16)
                    if first is None:
                        dve.wait_ge(s_pos, 4 * i + (2 * q + h - 1))
                    for b in range(HB):
                        nc.vector.scalar_tensor_tensor(junk[:, h, b, 0:(b + 1) * P], row[:, q, :, :].rearrange("p b e -> p (b e)")[:, h * HB * P:(h * HB + b + 1) * P],
                                                       M["dst2"][:, bass.ds(i * (2 * B) + (q * B + h * HB + b), 1)],
                                                       before[:, (HB - 1 - b) * P:], ALU.is_equal, ALU.mult,
                                                       accum_out=loc[:, h, b:b + 1]).then_inc(s_loc[q], 1)

                def use(i, q, h):
                    k = 4 * i + (2 * q + h)
                    dve.wait_ge(s_pr, k + 1)
                    nc.vector.tensor_tensor(sel[:, h, :, :], ps_pr[h][:, :, :], hot_hi[:, h, :, :], ALU.mult).then_inc(s_sel, 1)
                    dve.wait_ge(s_sel, k + 1)
                    nc.vector.tensor_reduce(prior[:, h, :], sel[:, h, :, :], AX.X, ALU.add).then_inc(s_prior, 1)
                    dve.wait_ge(s_prior, k + 1)
                    dve.wait_ge(s_put[q], i * (16 * B))
                    dve.wait_ge(s_loc[q], i * (2 * HB) + (h + 1) * HB)
                    nc.vector.tensor_tensor(pos[:, q, h * HB:(h + 1) * HB], prior[:, h, :], loc[:, h, :], ALU.add).then_inc(s_pos, 1)

                build(0, 0, 0, first=True)
                with dve.Fori(0, S2 // 2 - 1) as i:
                    for q in range(2):
                        build(i, q, 1)
                        use(i, q, 0)
                        build(i + q, 1 - q, 0)
                        use(i, q, 1)
                last = S2 // 2 - 1
                for q in range(2):
                    build(last, q, 1)
                    use(last, q, 0)
                    if q == 0:
                        build(last, 1, 0)
                    use(last, q, 1)


def over_groups(eng, body):
    with eng.Fori(0, NG // 2) as j:
        for b in range(2):
            body(j, b, G)
    body(NG // 2, 0, 1)


def mixer_context(nc, A, M):
    xn, stat, ident = M["xn"], M["stat"], M["ident"]
    HD = 32
    with ExitStack() as ctx:
        def sb(name, shape, dt=F32):
            return ctx.enter_context(nc.sbuf_tensor(name, shape, dt))

        sem = semaphores(nc, ctx)

        wx = sb("wx", [P, KD, D])
        bx = sb("bx", [P, KD])
        l1w = sb("l1w", [P, KD])
        l1b = sb("l1b", [P, KD])
        wkv = sb("wkv", [P, 2 * P])
        zer = sb("zer", [P, KD * (P + 1)])
        y = sb("y", [P, G, D])
        yT = sb("yT", [P, KD, G * P])
        xm = sb("xm", [P, 2, KD, G * P])
        kt = sb("kt", [P, KD, P])
        kmax = sb("kmax", [P, KD, P])
        top = sb("top", [P, KD, P])
        ke = sb("ke", [P, G, KD, P])
        vv = sb("vv", [P, G, KD, P + 1])
        blocks = sb("blocks", [P, P])
        rden = sb("rden", [P, KD])
        ps_y = ctx.enter_context(nc.psum_tensor("ps_y", [P, KD, G * P], F32))
        ps_x = ctx.enter_context(nc.psum_tensor("ps_x", [P, KD, G * P], F32))
        ps_k = ctx.enter_context(nc.psum_tensor("ps_k", [P, G, P], F32))
        ps_kv = [ctx.enter_context(nc.psum_tensor(f"ps_kv{b}", [P, KD, 2 * P], F32)) for b in range(2)]
        ps_c = ctx.enter_context(nc.psum_tensor("ps_c", [P, KD, P + 1], F32))

        s_w = sem("s_wm")
        s_z = sem("s_z")
        s_bd = sem("s_bd")
        s_y = sem("s_y")
        s_yt = sem("s_yt")
        s_yc = sem("s_yc")
        s_xm = sem("s_xm")
        s_xc = sem("s_xc")
        s_st = [sem(f"s_st{b}") for b in range(2)]
        s_k = sem("s_k")
        s_kr = sem("s_kr")
        s_km = sem("s_km")
        s_top = sem("s_top")
        s_ld = [sem(f"s_ld{b}") for b in range(2)]
        s_rd = [sem(f"s_rd{b}") for b in range(2)]
        s_kv = [sem(f"s_kv{b}") for b in range(2)]
        s_sub = [sem(f"s_sub{b}") for b in range(2)]
        s_v = [sem(f"s_v{b}") for b in range(2)]
        s_ke = [sem(f"s_ke{b}") for b in range(2)]
        s_c = sem("s_c")
        s_fin = sem("s_fin")

        with nc.Block() as block:
            @block.sync
            def _(sp):
                sp.dma_start(wx[:, :, :], A["WxT"].rearrange("(k p) n -> p k n", p=P)).then_inc(s_w, 16)
                for t, name in ((bx, "bx"), (l1w, "l1w"), (l1b, "l1b")):
                    sp.dma_start(t[:, :], A[name]).then_inc(s_w, 16)
                sp.wait_ge(s_z, 1)
                for a in range(0, P, HD):
                    sp.dma_start(wkv[a:a + HD, a:a + HD], A["WkT"]).then_inc(s_bd, 16)
                    sp.dma_start(wkv[a:a + HD, P + a:P + a + HD], A["WvT"]).then_inc(s_bd, 16)
                    sp.dma_start(M["wq"][a:a + HD, a:a + HD], A["WqT"]).then_inc(s_bd, 16)

                def store(j, b, T):
                    sp.wait_ge(s_xc, j * (2 * KD) + (b + 1) * KD)
                    sp.dma_start(M["xm_dram"][:, :, bass.ds((j * 2 + b) * (G * P), T * P)], xm[:, b, :, 0:T * P]).then_inc(s_st[b], 16)

                def load(j, b, T):
                    sp.wait_ge(s_rd[b], j)
                    sp.dma_start(xm[:, b, :, 0:T * P], M["xm_dram"][:, :, bass.ds((j * 2 + b) * (G * P), T * P)]).then_inc(s_ld[b], 16)

                over_groups(sp, store)
                sp.wait_ge(s_st[0], 16 * (NG // 2 + 1))
                sp.wait_ge(s_st[1], 16 * (NG // 2))
                sp.wait_ge(s_top, 1)
                over_groups(sp, load)

            @block.gpsimd
            def _(pool):
                pool.wait_ge(s_km, KD * (NG + 1))
                nc.gpsimd.partition_all_reduce(top[:, :, :].rearrange("p c s -> p (c s)"), kmax[:, :, :].rearrange("p c s -> p (c s)"),
                                               P, bass.bass_isa.ReduceOp.max).then_inc(s_top, 1)

            @block.tensor
            def _(pe):
                pe.wait_ge(s_w, 64)
                pe.wait_ge(s_bd, 16 * 3 * P // HD)

                def first(j, b, T):
                    i = j * 2 + b
                    pe.wait_ge(s_y, i + 1)
                    pe.wait_ge(s_yc, KD * i)
                    for t in range(T):
                        for k in range(KD):
                            m = pe.transpose(ps_y[:, k, t * P:(t + 1) * P], y[:, t, k * P:(k + 1) * P], ident[:, :])
                    m.then_inc(s_yt, 1)
                    pe.wait_ge(s_yc, KD * i + KD)
                    pe.wait_ge(s_xc, KD * i)
                    for o in range(KD):
                        for k in range(KD):
                            m = pe.matmul(ps_x[:, o, 0:T * P], wx[:, k, o * P:(o + 1) * P], yT[:, k, 0:T * P], start=(k == 0), stop=(k == KD - 1))
                        m.then_inc(s_xm, 1)
                    for c in range(KD):
                        pe.wait_ge(s_xc, KD * i + (c + 1))
                        pe.wait_ge(s_kr, KD * i + c)
                        for t in range(T):
                            m = pe.matmul(ps_k[:, t, :], xm[:, b, c, t * P:(t + 1) * P], wkv[:, 0:P], start=True, stop=True)
                        m.then_inc(s_k, 1)

                over_groups(pe, first)
                pe.wait_ge(s_z, 1)
                pe.matmul(ps_c[:, :, :].rearrange("p c n -> p (c n)"), zer[:, 0:P], zer[:, :], start=True, stop=False, skip_group_check=True)

                def second(j, b, T):
                    i = j * 2 + b
                    full = P if T == G else LAST

                    def context(t):
                        pe.wait_ge(s_ke[t % 2], i * 2 + (t // 2 + 1))
                        pe.wait_ge(s_v[t % 2], i * 2 + (t // 2 + 1))
                        for c in range(KD):
                            m = pe.matmul(ps_c[:, c, :], ke[0:full, t, c, :], vv[0:full, t, c, :], start=False, stop=False, skip_group_check=True)
                            if t == T - 1 and c == 0:
                                m.then_inc(s_rd[b], 1)
                        m.then_inc(s_c, 1)

                    pe.wait_ge(s_ld[b], j * 16 + 16)
                    for t in range(T):
                        pe.wait_ge(s_sub[t % 2], i * 2 + t // 2)
                        pe.wait_ge(s_v[t % 2], i * 2 + t // 2)
                        for c in range(KD):
                            m = pe.matmul(ps_kv[t % 2][:, c, :], xm[:, b, c, t * P:(t + 1) * P], wkv[:, :], start=True, stop=True)
                        m.then_inc(s_kv[t % 2], 1)
                        if t >= 1:
                            context(t - 1)
                    context(T - 1)

                over_groups(pe, second)

            @block.scalar
            def _(act):
                def first(j, b, T):
                    i = j * 2 + b
                    act.wait_ge(s_yt, i + 1)
                    act.wait_ge(s_xm, KD * i)
                    for k in range(KD):
                        nc.scalar.activation(yT[:, k, 0:T * P], ps_y[:, k, 0:T * P], ACT.Identity,
                                             bias=l1b[:, k:k + 1], scale=l1w[:, k:k + 1]).then_inc(s_yc, 1)
                    act.wait_ge(s_st[b], 16 * j)
                    for o in range(KD):
                        act.wait_ge(s_xm, KD * i + (o + 1))
                        nc.scalar.activation(xm[:, b, o, 0:T * P], ps_x[:, o, 0:T * P], ACT.Identity, bias=bx[:, o:o + 1]).then_inc(s_xc, 1)

                over_groups(act, first)

                def second(j, b, T):
                    i = j * 2 + b
                    for t in range(T):
                        act.wait_ge(s_sub[t % 2], i * 2 + (t // 2 + 1))
                        nc.scalar.activation(ke[:, t, :, :], ke[:, t, :, :], ACT.Exp).then_inc(s_ke[t % 2], 1)

                over_groups(act, second)

            @block.vector
            def _(dve):
                nc.vector.memset(wkv[:, :], 0.0)
                nc.vector.memset(M["wq"][:, :], 0.0)
                nc.vector.memset(zer[:, :], 0.0)
                nc.vector.memset(vv[:, :, :, P:P + 1], 1.0)
                nc.vector.memset(kmax[:, :, :], -3e38)
                nc.vector.memset(blocks[:, :], 0.0).then_inc(s_z, 1)
                dve.wait_ge(s_z, 1)
                for a in range(0, P, HD):
                    m = nc.vector.memset(blocks[a:a + HD, a:a + HD], 1.0)
                m.then_inc(s_fin, 1)

                def first(j, b, T):
                    i = j * 2 + b
                    dve.wait_ge(s_yt, i)
                    for t in range(T):
                        n = i * G + t
                        m = nc.vector.tensor_scalar(y[:, t, :], xn[:, n, :], stat[:, n, 0:1], stat[:, n, 1:2], ALU.subtract, ALU.mult)
                    m.then_inc(s_y, 1)
                    full = P if T == G else LAST
                    for c in range(KD):
                        dve.wait_ge(s_k, KD * i + (c + 1))
                        dve.wait_ge(s_km, KD * i)
                        nc.vector.tensor_reduce(kt[0:full, c, :], ps_k[0:full, 0:T, :].rearrange("p t s -> p s t"), AX.X, ALU.max).then_inc(s_kr, 1)
                        dve.wait_ge(s_kr, KD * i + (c + 1))
                        nc.vector.tensor_tensor(kmax[0:full, c, :], kmax[0:full, c, :], kt[0:full, c, :], ALU.max).then_inc(s_km, 1)

                over_groups(dve, first)
                dve.wait_ge(s_top, 1)

                def second(j, b, T):
                    i = j * 2 + b
                    for t in range(T):
                        dve.wait_ge(s_kv[t % 2], i * 2 + (t // 2 + 1))
                        dve.wait_ge(s_c, i * G)
                        nc.vector.tensor_tensor(ke[:, t, :, :], ps_kv[t % 2][:, :, 0:P], top[:, :, :], ALU.subtract).then_inc(s_sub[t % 2], 1)
                        nc.vector.tensor_copy(vv[:, t, :, 0:P], ps_kv[t % 2][:, :, P:2 * P]).then_inc(s_v[t % 2], 1)

                over_groups(dve, second)
                dve.wait_ge(s_c, NG * G + 1)
                nc.vector.reciprocal(rden[:, :], ps_c[:, :, P]).then_inc(s_fin, 1)
                dve.wait_ge(s_fin, 2)
                for c in range(KD):
                    nc.vector.scalar_tensor_tensor(M["kv"][:, c, :], ps_c[:, c, 0:P], rden[:, c:c + 1], blocks[:, :], ALU.mult, ALU.mult)


class Steps:

    def __init__(self, eng, sem, turn, per, base=0):
        self.eng, self.sem, self.turn, self.per, self.base, self.n = eng, sem, turn, per, base, 0

    def done(self, ins):
        ins.then_inc(self.sem, 1)
        self.n += 1

    def last(self):
        self.eng.wait_ge(self.sem, self.base + self.turn * self.per + self.n)

    def end(self, full):
        assert not full or self.n == self.per, self.n


RSQRT_STEPS = 12


def rsqrt(nc, c, r, v, t, ri, sem):
    c.done(nc.vector.tensor_scalar(r, v, EPS, None, ALU.add))
    c.last()
    c.done(nc.vector.tensor_scalar(v, r, -0.5, None, ALU.mult))
    c.done(nc.vector.tensor_single_scalar(ri, r.bitcast(I32), 1, ALU.logical_shift_right))
    c.last()
    c.done(nc.vector.tensor_scalar(r.bitcast(I32), ri, -1.0, float(0x5F3759DF), ALU.mult, ALU.add))
    for step in range(3):
        c.last()
        c.done(nc.vector.tensor_tensor(t, r, r, ALU.mult))
        c.last()
        c.done(nc.vector.tensor_tensor(t, t, v, ALU.mult))
        c.last()
        m = nc.vector.scalar_tensor_tensor(r, t, 1.5, r, ALU.add, ALU.mult)
        if step < 2:
            c.done(m)
    m.then_inc(sem, 1)


def nodes(nc, A, M):
    xn, ident = M["xn"], M["ident"]
    HM = D // 32
    KH = HID // P
    with ExitStack() as ctx:
        def sb(name, shape, dt=F32):
            return ctx.enter_context(nc.sbuf_tensor(name, shape, dt))

        sem = semaphores(nc, ctx)

        gw1 = sb("gw1", [P, KD, D])
        gw2 = sb("gw2", [P, KD, D])
        wo = sb("wo", [P, KD, D])
        mw1 = sb("mw1", [P, KD, HID])
        mw2 = sb("mw2", [P, KH, D])
        wgat = sb("wgat", [P, KD, HC])
        gb1 = sb("gb1", [P, KD])
        l2w = sb("l2w", [P, KD])
        l2b = sb("l2b", [P, KD])
        mb1 = sb("mb1", [P, KH])
        gb2, bo, mb2, gg, gb = (sb(n + "_r", [P, D]) for n in ("gb2", "bo", "mb2", "gg", "gb"))
        att = sb("att", [P, 2, HC])
        xm = sb("xm2", [P, 2, KD, G * P])
        ag = sb("ag", [P, TABLES, G, D])
        xr = sb("xr", [P, G, D])
        z = sb("z", [P, G, D])
        zT = sb("zT", [P, KD, G * P])
        g1 = sb("g1", [P, KD, G * P])
        q = sb("q", [P, G, D])
        qm = sb("qm", [P, G * HM])
        qs = sb("qs", [P, G * HM])
        hg = sb("hg", [P, G, D])
        h = sb("h", [P, G, D])
        y2 = sb("y2", [P, G, D])
        hid = sb("hid", [P, KH, G * P])
        x3T = sb("x3T", [P, 2, KD, G * P])
        bst = sb("bst2", [P, 3, G, 6])
        mv = sb("mv2", [P, 3, G, 2])
        rs = sb("rs2", [P, 3, G])
        rt = sb("rt2", [P, 3, G])
        ri = sb("ri2", [P, 3, G], I32)
        ha = sb("ha", [P, G, 2, HC])
        ps_a = ctx.enter_context(nc.psum_tensor("ps_a2", [P, KD, G * P], F32))
        ps_b = ctx.enter_context(nc.psum_tensor("ps_b2", [P, KD, G * P], F32))
        ps_m = [ctx.enter_context(nc.psum_tensor(f"ps_m{b}", [P, G * P], F32)) for b in range(2)]
        ps_n = ctx.enter_context(nc.psum_tensor("ps_n", [P, G, D], F32))

        s_w = sem("s_w2")
        s_xm = [sem(f"s_xm2{b}") for b in range(2)]
        s_ag = sem("s_ag2")
        s_xr = sem("s_xr")
        s_pool = sem("s_pool2")
        s_dve = sem("s_dve2")
        s_pass2 = sem("s_pass2")
        s_rows = sem("s_rows")
        s_clear = sem("s_clear")
        s_z = sem("s_z2")
        s_ql = sem("s_ql")
        s_sub = sem("s_sub2")
        s_qe = sem("s_qe")
        s_q = sem("s_q")
        s_zt = sem("s_zt")
        s_ztc = sem("s_ztc")
        s_g1 = sem("s_g1")
        s_g1c = sem("s_g1c")
        s_qt = sem("s_qt")
        s_qtc = sem("s_qtc")
        s_go = sem("s_go")
        s_gr = sem("s_gr")
        s_at = sem("s_at")
        s_atc = sem("s_atc")
        s_o = sem("s_o")
        s_or = sem("s_or")
        s_rs = sem("s_rs")
        s_y2 = sem("s_y2")
        s_yt = sem("s_yt2")
        s_ytc = sem("s_ytc")
        s_m1 = sem("s_m1")
        s_ge = sem("s_ge")
        s_m2 = sem("s_m2")
        s_mr = sem("s_mr")
        s_gt = sem("s_gt")
        s_r3 = sem("s_r3")
        s_x3 = sem("s_x3")
        s_x3t = sem("s_x3t")
        s_x3c = sem("s_x3c")
        s_st = [sem(f"s_st2{b}") for b in range(2)]
        s_h = sem("s_h")
        s_hr = sem("s_hr")
        s_row = sem("s_row2")

        with nc.Block() as block:
            @block.sync
            def _(sp):
                for t, name in ((gw1, "gW1"), (gw2, "gW2"), (wo, "WoT"), (mw1, "mW1T"), (mw2, "mW2T"), (wgat, "Wgat")):
                    sp.dma_start(t[:, :, :], A[name].rearrange("(k p) n -> p k n", p=P)).then_inc(s_w, 16)
                for t, name in ((gb1, "gb1"), (l2w, "l2w"), (l2b, "l2b"), (mb1, "mb1")):
                    sp.dma_start(t[:, :], A[name]).then_inc(s_w, 16)
                for t, name in ((gb2, "gb2"), (bo, "bo"), (mb2, "mb2"), (gg, "gg"), (gb, "gb")):
                    sp.dma_start(t[:, :], A[name].partition_broadcast(P)).then_inc(s_w, 16)
                for c, name in enumerate(("asrc", "adst")):
                    sp.dma_start(att[:, c, :], A[name].rearrange("h e -> (h e)").partition_broadcast(P)).then_inc(s_w, 16)

                def move(j, b, T):
                    i = j * 2 + b
                    sp.wait_ge(s_st[b], 16 * j)
                    sp.dma_start(xm[:, b, :, 0:T * P], M["xm_dram"][:, :, bass.ds(i * (G * P), T * P)]).then_inc(s_xm[b], 16)
                    rows = T * P if T == G else LAST
                    if T == 1:
                        sp.wait_ge(s_clear, 2)
                    r = P if T == G else LAST
                    sp.wait_ge(s_z, i)
                    for t in range(TABLES):
                        sp.dma_start(ag[0:r, t, 0:T, :], M["agg"][t][bass.ds(i * (G * P), rows), :].rearrange("(t p) d -> p t d", p=r)).then_inc(s_ag, 16)
                    sp.wait_ge(s_gt, i)
                    sp.dma_start(xr[0:r, 0:T, :], A["x"][bass.ds(i * (G * P), rows), :].rearrange("(t p) d -> p t d", p=r)).then_inc(s_xr, 16)

                over_groups(sp, move)

            @block.gpsimd
            def _(pool):
                pool.wait_ge(s_w, 16 * 17)

                def group(j, b, T):
                    i = j * 2 + b
                    r = P if T == G else LAST
                    c = Steps(pool, s_pool, i, 5 + G)
                    if T == 1:
                        pool.wait_ge(s_gt, NG)
                        nc.gpsimd.memset(ag[:, :, 0, :], 0.0).then_inc(s_clear, 1)
                        nc.gpsimd.memset(xr[:, 0, :], 0.0).then_inc(s_clear, 1)
                    pool.wait_ge(s_ag, i * (16 * TABLES) + 16 * TABLES)
                    c.done(nc.gpsimd.tensor_tensor(ag[:, 0, 0:T, :], ag[:, 0, 0:T, :], ag[:, 1, 0:T, :], ALU.add))
                    c.done(nc.gpsimd.tensor_tensor(ag[:, 2, 0:T, :], ag[:, 2, 0:T, :], ag[:, 3, 0:T, :], ALU.add))
                    c.last()
                    c.done(nc.gpsimd.tensor_tensor(ag[:, 0, 0:T, :], ag[:, 0, 0:T, :], ag[:, 2, 0:T, :], ALU.add))
                    c.last()
                    pool.wait_ge(s_zt, i)
                    nc.gpsimd.tensor_tensor(z[:, 0:T, :], ag[:, 0, 0:T, :], xn[:, bass.ds(i * G, T), :], ALU.add).then_inc(s_z, 1)
                    pool.wait_ge(s_rs, i + 1)
                    pool.sem_inc(s_pass2, 1)
                    for t in range(T):
                        c.done(nc.gpsimd.tensor_scalar(hg[:, t, :], hg[:, t, :], mv[:, 0, t, 0:1], rs[:, 0, t:t + 1], ALU.subtract, ALU.mult))
                    c.last()
                    c.done(nc.gpsimd.tensor_tensor(hg[:, 0:T, :], hg[:, 0:T, :], gg[:, None, :].broadcast_to([P, T, D]), ALU.mult))
                    c.last()
                    c.done(nc.gpsimd.tensor_tensor(hg[:, 0:T, :], hg[:, 0:T, :], gb[:, None, :].broadcast_to([P, T, D]), ALU.add))
                    c.last()
                    pool.wait_ge(s_xr, i * 16 + 16)
                    nc.gpsimd.tensor_tensor(hg[:, 0:T, :], hg[:, 0:T, :], xr[:, 0:T, :], ALU.add).then_inc(s_gt, 1)
                    c.end(T == G)

                over_groups(pool, group)

            @block.tensor
            def _(pe):
                pe.wait_ge(s_w, 16 * 17)

                def turn(dst, src, T, s):
                    for t in range(T):
                        for k in range(KD):
                            m = pe.transpose(dst[:, k, t * P:(t + 1) * P], src[:, t, k * P:(k + 1) * P], ident[:, :])
                    m.then_inc(s, 1)

                def group(j, b, T):
                    i = j * 2 + b
                    w = T * P
                    pe.wait_ge(s_xm[b], j * 16 + 16)
                    pe.wait_ge(s_mr, i)
                    for t in range(T):
                        for k in range(KD):
                            m = pe.matmul(ps_n[:, t, k * P:(k + 1) * P], xm[:, b, k, t * P:(t + 1) * P], M["wq"][:, :], start=True, stop=True)
                    m.then_inc(s_ql, 1)
                    pe.wait_ge(s_z, i + 1)
                    pe.wait_ge(s_x3c, i)
                    turn(ps_a, z, T, s_zt)
                    pe.wait_ge(s_ztc, i + 1)
                    pe.wait_ge(s_hr, i)
                    for o in range(KD):
                        for k in range(KD):
                            m = pe.matmul(ps_b[:, o, 0:w], gw1[:, k, o * P:(o + 1) * P], zT[:, k, 0:w], start=(k == 0), stop=(k == KD - 1))
                    m.then_inc(s_g1, 1)
                    pe.wait_ge(s_q, i + 1)
                    turn(ps_a, q, T, s_qt)
                    pe.wait_ge(s_g1c, i + 1)
                    for t in range(T):
                        for k in range(KD):
                            m = pe.matmul(ps_n[:, t, :], g1[:, k, t * P:(t + 1) * P], gw2[:, k, :], start=(k == 0), stop=(k == KD - 1))
                    m.then_inc(s_go, 1)
                    pe.wait_ge(s_qtc, i + 1)
                    for k in range(KD):
                        m = pe.matmul(ps_b[:, k, 0:w], M["kv"][:, k, :], zT[:, k, 0:w], start=True, stop=True)
                    m.then_inc(s_at, 1)
                    pe.wait_ge(s_atc, i + 1)
                    pe.wait_ge(s_gr, i + 1)
                    for t in range(T):
                        for k in range(KD):
                            m = pe.matmul(ps_n[:, t, :], g1[:, k, t * P:(t + 1) * P], wo[:, k, :], start=(k == 0), stop=(k == KD - 1))
                    m.then_inc(s_o, 1)
                    pe.wait_ge(s_y2, i + 1)
                    turn(ps_a, y2, T, s_yt)
                    pe.wait_ge(s_ytc, i + 1)
                    for c in range(KH):
                        pe.wait_ge(s_ge, KH * i + max(c - 1, 0))
                        for k in range(KD):
                            m = pe.matmul(ps_m[c % 2][:, 0:w], mw1[:, k, c * P:(c + 1) * P], zT[:, k, 0:w], start=(k == 0), stop=(k == KD - 1))
                        m.then_inc(s_m1, 1)
                    pe.wait_ge(s_ge, KH * i + KH)
                    pe.wait_ge(s_or, i + 1)
                    for t in range(T):
                        for c in range(KH):
                            m = pe.matmul(ps_n[:, t, :], hid[:, c, t * P:(t + 1) * P], mw2[:, c, :], start=(c == 0), stop=(c == KH - 1))
                    m.then_inc(s_m2, 1)
                    pe.wait_ge(s_x3, i + 1)
                    turn(ps_a, y2, T, s_x3t)
                    pe.wait_ge(s_x3c, i + 1)
                    for t in range(T):
                        for k in range(KD):
                            m = pe.matmul(ps_b[:, 0, t * HC:(t + 1) * HC], x3T[:, b, k, t * P:(t + 1) * P], wgat[:, k, :], start=(k == 0), stop=(k == KD - 1))
                    m.then_inc(s_h, 1)

                over_groups(pe, group)

            @block.scalar
            def _(act):
                def group(j, b, T):
                    i = j * 2 + b
                    w = T * P
                    act.wait_ge(s_sub, i + 1)
                    nc.scalar.activation(q[:, 0:T, :], q[:, 0:T, :], ACT.Exp).then_inc(s_qe, 1)
                    act.wait_ge(s_zt, i + 1)
                    for k in range(KD):
                        m = nc.scalar.activation(zT[:, k, 0:w], ps_a[:, k, 0:w], ACT.Copy)
                    m.then_inc(s_ztc, 1)
                    act.wait_ge(s_g1, i + 1)
                    for k in range(KD):
                        m = nc.scalar.activation(g1[:, k, 0:w], ps_b[:, k, 0:w], ACT.Relu, bias=gb1[:, k:k + 1])
                    m.then_inc(s_g1c, 1)
                    act.wait_ge(s_qt, i + 1)
                    for k in range(KD):
                        m = nc.scalar.activation(zT[:, k, 0:w], ps_a[:, k, 0:w], ACT.Copy)
                    m.then_inc(s_qtc, 1)
                    act.wait_ge(s_at, i + 1)
                    for k in range(KD):
                        m = nc.scalar.activation(g1[:, k, 0:w], ps_b[:, k, 0:w], ACT.Copy)
                    m.then_inc(s_atc, 1)
                    act.wait_ge(s_yt, i + 1)
                    for k in range(KD):
                        m = nc.scalar.activation(zT[:, k, 0:w], ps_a[:, k, 0:w], ACT.Identity, bias=l2b[:, k:k + 1], scale=l2w[:, k:k + 1])
                    m.then_inc(s_ytc, 1)
                    for c in range(KH):
                        act.wait_ge(s_m1, KH * i + (c + 1))
                        nc.scalar.activation(hid[:, c, 0:w], ps_m[c % 2][:, 0:w], ACT.Gelu, bias=mb1[:, c:c + 1]).then_inc(s_ge, 1)
                    act.wait_ge(s_x3t, i + 1)
                    act.wait_ge(s_st[b], 16 * j)
                    for k in range(KD):
                        m = nc.scalar.activation(x3T[:, b, k, 0:w], ps_a[:, k, 0:w], ACT.Copy)
                    m.then_inc(s_x3c, 1)
                    act.wait_ge(s_x3c, i + 1)
                    act.dma_start(M["x3T_dram"][:, :, bass.ds(i * (G * P), w)], x3T[:, b, :, 0:w]).then_inc(s_st[b], 16)

                act.wait_ge(s_w, 16 * 17)
                over_groups(act, group)
                act.wait_ge(s_st[0], 16 * (NG // 2 + 1))
                act.wait_ge(s_st[1], 16 * (NG // 2))
                act.wait_ge(s_rows, 1)
                act.dma_start(M["row_dram"].rearrange("(t p) c -> p t c", p=P), M["rows"][:, :, :]).then_inc(s_row, 16)
                act.wait_ge(s_row, 16)

            @block.vector
            def _(dve):
                dve.wait_ge(s_w, 16 * 17)

                def group(j, b, T):
                    i = j * 2 + b
                    here = bass.ds(i * G, T)
                    c = Steps(dve, s_dve, i, 11 + 6 * G + 2 * RSQRT_STEPS)

                    def moments(x, n):
                        for t in range(T):
                            c.done(nc.vector.bn_stats(bst[:, n, t, :], x[:, t, :]))
                        c.last()
                        dve.sem_inc(s_pass2, 1)

                    def close(n):
                        for t in range(T):
                            c.done(nc.vector.bn_aggr(mv[:, n, t, :], bst[:, n, t, :]))

                    logits = ps_n[:, 0:T, :].rearrange("p t (m s) -> p (t m) s", s=32)
                    qh = q[:, 0:T, :].rearrange("p t (m s) -> p (t m) s", s=32)
                    n = T * HM
                    dve.wait_ge(s_ql, i + 1)
                    c.done(nc.vector.tensor_reduce(qm[:, 0:n], logits, AX.X, ALU.max))
                    c.last()
                    dve.wait_ge(s_qt, i)
                    nc.vector.tensor_tensor(qh, logits, qm[:, 0:n, None].broadcast_to([P, n, 32]), ALU.subtract).then_inc(s_sub, 1)
                    dve.wait_ge(s_qe, i + 1)
                    c.done(nc.vector.tensor_reduce(qs[:, 0:n], qh, AX.X, ALU.add))
                    c.last()
                    c.done(nc.vector.reciprocal(qs[:, 0:n], qs[:, 0:n]))
                    c.last()
                    nc.vector.tensor_tensor(qh, qh, qs[:, 0:n, None].broadcast_to([P, n, 32]), ALU.mult).then_inc(s_q, 1)
                    dve.wait_ge(s_go, i + 1)
                    nc.vector.tensor_tensor(hg[:, 0:T, :], ps_n[:, 0:T, :], gb2[:, None, :].broadcast_to([P, T, D]), ALU.add).then_inc(s_gr, 1)
                    dve.wait_ge(s_gr, i + 1)
                    c.done(nc.vector.scalar_tensor_tensor(hg[:, 0:T, :], hg[:, 0:T, :], 0.0, xn[:, here, :], ALU.max, ALU.add))
                    c.last()
                    moments(hg, 0)
                    close(0)
                    dve.wait_ge(s_o, i + 1)
                    nc.vector.tensor_tensor(h[:, 0:T, :], ps_n[:, 0:T, :], bo[:, None, :].broadcast_to([P, T, D]), ALU.add).then_inc(s_or, 1)
                    dve.wait_ge(s_or, i + 1)
                    c.done(nc.vector.tensor_tensor(h[:, 0:T, :], h[:, 0:T, :], xn[:, here, :], ALU.add))
                    c.last()
                    moments(h, 1)
                    close(1)
                    c.last()
                    rsqrt(nc, c, rs[:, 0:2, 0:T], mv[:, 0:2, 0:T, 1], rt[:, 0:2, 0:T], ri[:, 0:2, 0:T], s_rs)
                    dve.wait_ge(s_rs, i + 1)
                    for t in range(T):
                        m = nc.vector.tensor_scalar(y2[:, t, :], h[:, t, :], mv[:, 1, t, 0:1], rs[:, 1, t:t + 1], ALU.subtract, ALU.mult)
                    m.then_inc(s_y2, 1)
                    dve.wait_ge(s_m2, i + 1)
                    c.done(nc.vector.tensor_tensor(h[:, 0:T, :], h[:, 0:T, :], mb2[:, None, :].broadcast_to([P, T, D]), ALU.add))
                    c.last()
                    nc.vector.tensor_tensor(h[:, 0:T, :], ps_n[:, 0:T, :], h[:, 0:T, :], ALU.add).then_inc(s_mr, 1)
                    dve.wait_ge(s_mr, i + 1)
                    dve.wait_ge(s_gt, i + 1)
                    c.done(nc.vector.tensor_tensor(xn[:, here, :], h[:, 0:T, :], hg[:, 0:T, :], ALU.add))
                    c.done(nc.vector.tensor_tensor(h[:, 0:T, :], h[:, 0:T, :], hg[:, 0:T, :], ALU.add))
                    c.last()
                    moments(h, 2)
                    close(2)
                    c.last()
                    rsqrt(nc, c, rs[:, 2, 0:T], mv[:, 2, 0:T, 1], rt[:, 2, 0:T], ri[:, 2, 0:T], s_r3)
                    dve.wait_ge(s_r3, i + 1)
                    for t in range(T):
                        m = nc.vector.tensor_scalar(y2[:, t, :], h[:, t, :], mv[:, 2, t, 0:1], rs[:, 2, t:t + 1], ALU.subtract, ALU.mult)
                    m.then_inc(s_x3, 1)
                    dve.wait_ge(s_h, i + 1)
                    ph = ps_b[:, 0, 0:T * HC].rearrange("p (t c) -> p t c", c=HC)
                    c.done(nc.vector.tensor_copy(M["rows"][:, here, HEADS:ROWC], ph))
                    for a in range(2):
                        m = nc.vector.tensor_tensor(ha[:, 0:T, a, :], ph, att[:, a, None, :].broadcast_to([P, T, HC]), ALU.mult)
                    m.then_inc(s_hr, 1)
                    dve.wait_ge(s_hr, i + 1)
                    for a, dst in ((0, M["rows"][:, here, 0:HEADS]), (1, M["adst"][:, here, :])):
                        c.done(nc.vector.tensor_reduce(dst, ha[:, 0:T, a, :].rearrange("p t (m e) -> p t m e", e=NE), AX.X, ALU.add))
                    c.last()
                    c.end(T == G)

                over_groups(dve, group)
                dve.sem_inc(s_rows, 1)


def gat_edges_and_experts(nc, A, M):
    R = 2
    KE = EH // P
    with ExitStack() as ctx:
        def sb(name, shape, dt=F32):
            return ctx.enter_context(nc.sbuf_tensor(name, shape, dt))

        sem = semaphores(nc, ctx)

        order = sb("order_sb", [P, S3, MB], I32)
        gi = sb("gi2", [P, R, MB], I32)
        er = sb("er2", [P, R, MB, ROWC])
        w1 = sb("ew1", [P, NE, KD, EH])
        w2 = sb("ew2", [P, NE, KE, D])
        b1 = sb("eb1", [P, NE * KE])
        b2 = sb("eb2_r", [P, NE, D])
        xT = sb("xT4", [P, 2, KD, G * P])
        hid = sb("hid4", [P, 2, KE, G * P])
        eo = sb("eo4", [P, 2, G, D])
        ps_m = [ctx.enter_context(nc.psum_tensor(f"ps_em{c}", [P, G * P], F32)) for c in range(KE)]
        ps_n = [ctx.enter_context(nc.psum_tensor(f"ps_en{c}", [P, G, D], F32)) for c in range(2)]

        s_idx = [sem(f"s_ei{r}") for r in range(R)]
        s_get = [sem(f"s_get{r}") for r in range(R)]
        s_put = [sem(f"s_put{r}") for r in range(R)]
        s_ord = sem("s_ord")
        s_go = sem("s_go4")
        s_w = sem("s_w4")
        s_x = [sem(f"s_x4{b}") for b in range(2)]
        s_m = sem("s_m4")
        s_ge = sem("s_ge4")
        s_n = [sem(f"s_n4{b}") for b in range(2)]
        s_e = sem("s_e4")
        s_st = [sem(f"s_st4{b}") for b in range(2)]

        with nc.Block() as block:
            @block.gpsimd
            def _(pool):
                def stage(j, r):
                    pool.wait_ge(s_put[r], j * 16)
                    nc.gpsimd.tensor_copy(gi[:, r, :], order[:, j * R + r, :]).then_inc(s_idx[r], 1)

                def gather(j, r):
                    pool.wait_ge(s_idx[r], j + 1)
                    pool.sem_inc(s_go, 1)
                    for b in range(MB):
                        pool.indirect_dma_start(er[:, r, b, :], None, M["row_dram"],
                                                bass.IndirectOffsetOnAxis(ap=gi[:, r, b:b + 1], axis=0)).then_inc(s_get[r], 16)

                def store(j, r):
                    pool.wait_ge(s_get[r], j * (16 * MB) + 16 * MB)
                    pool.dma_start(M["erow"][bass.ds((j * R + r) * (P * MB * ROWC), P * MB * ROWC), :].rearrange("(p n) o -> p (n o)", p=P),
                                   er[:, r, :, :].rearrange("p b c -> p (b c)")).then_inc(s_put[r], 16)

                pool.dma_start(order[:, :, :], M["order"].rearrange("(s p b) o -> p s (b o)", p=P, b=MB)).then_inc(s_ord, 16)
                pool.wait_ge(s_ord, 16)
                stage(0, 0)
                gather(0, 0)
                with pool.Fori(0, S3 // R - 1) as j:
                    stage(j, 1)
                    gather(j, 1)
                    store(j, 0)
                    stage(j + 1, 0)
                    gather(j + 1, 0)
                    store(j, 1)
                last = S3 // R - 1
                stage(last, 1)
                gather(last, 1)
                store(last, 0)
                store(last, 1)
                for r in range(R):
                    pool.wait_ge(s_put[r], 16 * (last + 1))

            @block.sync
            def _(sp):
                for e in range(NE):
                    sp.dma_start(w1[:, e, :, :], A["eW1"][e].rearrange("(k p) n -> p k n", p=P)).then_inc(s_w, 16)
                    sp.dma_start(w2[:, e, :, :], A["eW2"][e].rearrange("(k p) n -> p k n", p=P)).then_inc(s_w, 16)
                    sp.dma_start(b2[:, e, :], A["eb2"][e].partition_broadcast(P)).then_inc(s_w, 16)
                sp.dma_start(b1[:, :], A["eb1"]).then_inc(s_w, 16)

                def store(j, b, T):
                    i = j * 2 + b
                    for e in range(NE):
                        sp.wait_ge(s_e, i * NE + (e + 1))
                        sp.dma_start(M["eo_dram"][e][bass.ds(i * (G * P), T * P), :].rearrange("(t p) d -> p t d", p=P),
                                     eo[:, e % 2, 0:T, :]).then_inc(s_st[e % 2], 16)

                over_groups(sp, store)
                for b in range(2):
                    sp.wait_ge(s_st[b], 16 * (NE // 2) * (NG + 1))

            @block.tensor
            def _(pe):
                pe.wait_ge(s_w, 16 * (3 * NE + 1))

                def group(j, b, T):
                    i = j * 2 + b
                    w = T * P

                    def up(e):
                        for c in range(KE):
                            n = (e - 1) * KE + c + 1
                            pe.wait_ge(s_ge, i * (NE * KE) + n if e else i * (NE * KE))
                            for k in range(KD):
                                m = pe.matmul(ps_m[c][:, 0:w], w1[:, e, k, c * P:(c + 1) * P], xT[:, b, k, 0:w], start=(k == 0), stop=(k == KD - 1))
                            m.then_inc(s_m, 1)

                    def down(e):
                        pe.wait_ge(s_ge, i * (NE * KE) + (e + 1) * KE)
                        pe.wait_ge(s_e, i * NE + max(e - 1, 0))
                        for t in range(T):
                            for c in range(KE):
                                m = pe.matmul(ps_n[e % 2][:, t, :], hid[:, e % 2, c, t * P:(t + 1) * P], w2[:, e, c, :], start=(c == 0), stop=(c == KE - 1))
                        m.then_inc(s_n[b], 1)

                    pe.wait_ge(s_x[b], j * 16 + 16)
                    up(0)
                    for e in range(NE):
                        if e + 1 < NE:
                            up(e + 1)
                        down(e)

                over_groups(pe, group)

            @block.scalar
            def _(act):
                act.wait_ge(s_w, 16 * (3 * NE + 1))

                def group(j, b, T):
                    i = j * 2 + b
                    w = T * P
                    act.wait_ge(s_n[b], j * NE)
                    act.dma_start(xT[:, b, :, 0:w], M["x3T_dram"][:, :, bass.ds(i * (G * P), w)]).then_inc(s_x[b], 16)
                    for e in range(NE):
                        if e >= 2:
                            act.wait_ge(s_n[b], j * NE + (e - 1))
                        elif b == 1:
                            act.wait_ge(s_n[0], j * NE + (NE + e - 1))
                        elif T == G:
                            act.wait_ge(s_n[1], j * NE)
                        else:
                            act.wait_ge(s_n[1], j * NE)
                        for c in range(KE):
                            act.wait_ge(s_m, i * (NE * KE) + (e * KE + c + 1))
                            nc.scalar.activation(hid[:, e % 2, c, 0:w], ps_m[c][:, 0:w], ACT.Gelu,
                                                 bias=b1[:, e * KE + c:e * KE + c + 1]).then_inc(s_ge, 1)

                over_groups(act, group)

            @block.vector
            def _(dve):
                dve.wait_ge(s_w, 16 * (3 * NE + 1))

                def group(j, b, T):
                    i = j * 2 + b
                    for e in range(NE):
                        dve.wait_ge(s_n[b], j * NE + (e + 1))
                        dve.wait_ge(s_st[e % 2], i * (16 * NE // 2) + 16 * (e // 2))
                        nc.vector.tensor_tensor(eo[:, e % 2, 0:T, :], ps_n[e % 2][:, 0:T, :], b2[:, e, None, :].broadcast_to([P, T, D]), ALU.add).then_inc(s_e, 1)

                over_groups(dve, group)


def attend_and_combine(nc, A, M, out):
    K = SLOTS
    with ExitStack() as ctx:
        def sb(name, shape, dt=F32):
            return ctx.enter_context(nc.sbuf_tensor(name, shape, dt))

        sem = semaphores(nc, ctx)

        el = sb("el", [P, 2, G, K * ROWC])
        start = sb("start5", [P, NT])
        starti = sb("starti5", [P, NT], I32)
        at = sb("at5", [P, 2, G], I32)
        left = sb("left5", [P, NT])
        slot = sb("slot5", [P, K], I32)
        slotf = sb("slotf5", [P, K])
        mask = sb("mask5", [P, NT, K])
        e = sb("e5", [P, G, K + 1, HEADS])
        mn = sb("mn", [P, G, HEADS])
        ds = sb("ds5", [P, G, HEADS])
        pr = sb("pr5", [P, G, K, HC])
        dg = sb("dg5", [P, G, HC])
        m = sb("m5", [P, NT, HEADS])
        den = sb("den5", [P, NT, HEADS])
        agg = sb("agg5", [P, NT, HC])
        bgat, fg, fb = (sb(n + "_r5", [P, HC]) for n in ("bgat", "fg", "fb"))
        a1 = sb("a15", [P, NT, HC])
        v = sb("v5", [P, NT])
        r = sb("r5", [P, NT])
        t1 = sb("t15", [P, NT])
        ri = sb("ri5", [P, NT], I32)
        sc = sb("sc5", [P, NT, NE])
        wins = sb("wins5", [P, NT, NE, NE])
        ties = sb("ties5", [P, NT, NE, NE])
        low = sb("low5", [P, NE, NE])
        sel = sb("sel5", [P, NT, NE])
        g = sb("g5", [P, NT, NE])
        eo = sb("eo5", [P, 2, NE, G, D])
        acc = sb("acc5", [P, 2, G, D])

        s_w = sem("s_w5")
        s_iota = sem("s_iota5")
        s_round = sem("s_round5")
        s_at = sem("s_at5")
        s_el = [sem(f"s_el{b}") for b in range(2)]
        s_eo = [sem(f"s_eo{b}") for b in range(2)]
        s_d = sem("s_d5")
        s_dl = sem("s_dl5")
        s_dr = sem("s_dr5")
        s_dc = sem("s_dc5")
        s_sub = sem("s_sub5")
        s_exp = sem("s_exp5")
        s_read = sem("s_read5")
        s_gs = sem("s_gs5")
        s_ge = sem("s_ge5")
        s_out = sem("s_out5")
        s_st = [sem(f"s_st5{b}") for b in range(2)]
        s_go = sem("s_go5")

        def rounds(eng):
            most = nc.values_load(M["mosti"][0:1, 0:1], engines=[eng.engine], min_val=0, max_val=E2,
                                  skip_runtime_bounds_check_because="it is a number of in-edges, of which there are E2")
            return (most + (SLOTS - 1)) // SLOTS

        with nc.Block() as block:
            @block.sync
            def _(sp):
                for t, name in ((bgat, "bgat"), (fg, "fg"), (fb, "fb")):
                    sp.dma_start(t[:, :], A[name].partition_broadcast(P)).then_inc(s_w, 16)
                def load(j, b, T):
                    i = j * 2 + b
                    sp.wait_ge(s_out, i - 1) if b else sp.wait_ge(s_out, i)
                    for x in range(NE):
                        sp.dma_start(eo[:, b, x, 0:T, :], M["eo_dram"][x][bass.ds(i * (G * P), T * P), :].rearrange("(t p) d -> p t d", p=P)).then_inc(s_eo[b], 16)

                over_groups(sp, load)

            @block.scalar
            def _(act):
                with act.Fori(0, rounds(act)) as turn:
                    def group(j, b, T):
                        act.wait_ge(s_sub, turn * (NG + 1) + (j * 2 + (b + 1)))
                        nc.scalar.activation(e[:, 0:T, :, :], e[:, 0:T, :, :], ACT.Exp).then_inc(s_exp, 1)

                    over_groups(act, group)
                act.wait_ge(s_gs, 1)
                nc.scalar.activation(g[:, :, :], g[:, :, :], ACT.Exp).then_inc(s_ge, 1)

                def put(j, b, T):
                    i = j * 2 + b
                    act.wait_ge(s_out, i + 1)
                    rows, p = (T * P, P) if T == G else (LAST, LAST)
                    act.dma_start(out[bass.ds(i * (G * P), rows), :].rearrange("(t p) d -> p t d", p=p), acc[0:p, b, 0:T, :]).then_inc(s_st[b], 16)

                over_groups(act, put)
                act.wait_ge(s_st[0], 16 * (NG // 2 + 1))
                act.wait_ge(s_st[1], 16 * (NG // 2))

            @block.gpsimd
            def _(pool):
                nc.gpsimd.iota(slot[:, :], pattern=[[1, K]], base=0, channel_multiplier=0).then_inc(s_iota, 1)
                with pool.Fori(0, rounds(pool)) as turn:
                    pool.wait_ge(s_round, turn + 1)
                    pool.sem_inc(s_go, 1)

                    def load(j, b, T):
                        i = turn * (NG + 1) + (j * 2 + b)
                        pool.wait_ge(s_read, i - 1) if b else pool.wait_ge(s_read, i)
                        pool.sem_inc(s_go, 1)
                        nc.gpsimd.tensor_copy(at[:, b, 0:T], starti[:, bass.ds(j * (2 * G) + b * G, T)]).then_inc(s_at, 1)
                        pool.wait_ge(s_at, i + 1)
                        pool.sem_inc(s_go, 1)
                        for t in range(T):
                            pool.indirect_dma_start(el[:, b, t, :], None, M["erow"],
                                                    bass.IndirectOffsetOnAxis(ap=at[:, b, t:t + 1], axis=0)).then_inc(s_el[b], 16)

                    over_groups(pool, load)

            @block.vector
            def _(dve):
                c = Chain(dve, s_d)
                a = M["rows"][:, :, 0:HEADS]
                for x in range(NE):
                    if x:
                        c.done(nc.vector.memset(low[:, x, 0:x], 1.0))
                    c.done(nc.vector.memset(low[:, x, x:], 0.0))
                c.done(nc.vector.tensor_tensor(den[:, :, :], a, M["adst"][:, :, :], ALU.add))
                c.done(nc.vector.tensor_copy(agg[:, :, :], M["rows"][:, :, HEADS:ROWC]))
                c.done(nc.vector.tensor_copy(start[:, :], M["off"][:, 0:NT]))
                c.done(nc.vector.tensor_copy(left[:, :], M["deg"][:, 0:NT]))
                dve.wait_ge(s_iota, 1)
                c.done(nc.vector.tensor_copy(slotf[:, :], slot[:, :]))
                c.last()
                c.done(nc.vector.scalar_tensor_tensor(m[:, :, :], den[:, :, :], 0.2, den[:, :, :], ALU.mult, ALU.max))
                c.last()
                c.done(nc.vector.memset(den[:, :, :], 1.0))
                c.last()

                with dve.Fori(0, rounds(dve)) as turn:
                    s = Steps(dve, s_dr, turn, 4)
                    nc.vector.tensor_scalar(starti[:, :], start[:, :], float(ROWC), None, ALU.mult).then_inc(s_round, 1)
                    s.done(nc.vector.tensor_tensor(mask[:, :, :], slotf[:, None, :].broadcast_to([P, NT, K]), left[:, :, None].broadcast_to([P, NT, K]), ALU.is_ge))
                    s.last()
                    dve.wait_ge(s_round, turn + 1)
                    s.done(nc.vector.tensor_scalar(mask[:, :, :], mask[:, :, :], PAD, None, ALU.mult))
                    s.done(nc.vector.tensor_scalar(start[:, :], start[:, :], float(K), float(E2), ALU.add, ALU.min))
                    s.done(nc.vector.tensor_scalar(left[:, :], left[:, :], -float(K), None, ALU.add))
                    s.last()
                    dve.sem_inc(s_go, 1)

                    def group(j, b, T):
                        n = j * 2 + b
                        i = turn * (NG + 1) + n
                        here = bass.ds(n * G, T)
                        full = 12 + G
                        s = Steps(dve, s_dl, n, full, base=turn * (NG * full + full + 1 - G))
                        row = el[:, b, 0:T, :].rearrange("p t (k c) -> p t k c", c=ROWC)
                        le = e[:, 0:T, 0:K, :]
                        dve.wait_ge(s_el[b], turn * (16 * (NG // 2 * G + 1 - b)) + j * (16 * G) + 16 * T)
                        s.done(nc.vector.tensor_tensor(le, row[:, :, :, 0:HEADS], M["adst"][:, here, :][:, :, None, :].broadcast_to([P, T, K, HEADS]), ALU.add))
                        s.last()
                        s.done(nc.vector.scalar_tensor_tensor(le, le, 0.2, le, ALU.mult, ALU.max))
                        s.last()
                        s.done(nc.vector.tensor_tensor(le, le, mask[:, here, :, None].broadcast_to([P, T, K, HEADS]), ALU.add))
                        s.last()
                        s.done(nc.vector.tensor_reduce(mn[:, 0:T, :], le.rearrange("p t k h -> p t h k"), AX.X, ALU.max))
                        s.last()
                        s.done(nc.vector.tensor_tensor(mn[:, 0:T, :], mn[:, 0:T, :], m[:, here, :], ALU.max))
                        s.last()
                        s.done(nc.vector.tensor_tensor(e[:, 0:T, K, :], m[:, here, :], mn[:, 0:T, :], ALU.subtract))
                        nc.vector.tensor_tensor(le, le, mn[:, 0:T, None, :].broadcast_to([P, T, K, HEADS]), ALU.subtract).then_inc(s_sub, 1)
                        dve.wait_ge(s_exp, i + 1)
                        s.done(nc.vector.tensor_reduce(ds[:, 0:T, :], le.rearrange("p t k h -> p t h k"), AX.X, ALU.add))
                        for t in range(T):
                            x = nc.vector.tensor_tensor(pr[:, t, :, :].rearrange("p k (h c) -> p k h c", c=NE),
                                                        el[:, b, t, :].rearrange("p (k c) -> p k c", c=ROWC)[:, :, HEADS:].rearrange("p k (h c) -> p k h c", c=NE),
                                                        e[:, t, 0:K, :, None].broadcast_to([P, K, HEADS, NE]), ALU.mult)
                            if t < T - 1:
                                s.done(x)
                        x.then_inc(s_read, 1)
                        scale = e[:, 0:T, K, :]
                        s.done(nc.vector.tensor_tensor(den[:, here, :], den[:, here, :], scale, ALU.mult))
                        s.done(nc.vector.tensor_tensor(agg[:, here, :].rearrange("p t (h c) -> p t h c", c=NE),
                                                       agg[:, here, :].rearrange("p t (h c) -> p t h c", c=NE),
                                                       scale[:, :, :, None].broadcast_to([P, T, HEADS, NE]), ALU.mult))
                        dve.wait_ge(s_read, i + 1)
                        s.done(nc.vector.tensor_reduce(dg[:, 0:T, :], pr[:, 0:T, :, :].rearrange("p t k c -> p t c k"), AX.X, ALU.add))
                        s.last()
                        s.done(nc.vector.tensor_tensor(den[:, here, :], den[:, here, :], ds[:, 0:T, :], ALU.add))
                        s.done(nc.vector.tensor_tensor(agg[:, here, :], agg[:, here, :], dg[:, 0:T, :], ALU.add))
                        s.done(nc.vector.tensor_copy(m[:, here, :], mn[:, 0:T, :]))
                        s.last()
                        s.end(T == G)

                    over_groups(dve, group)
                c.done(nc.vector.tensor_scalar(den[:, :, :], den[:, :, :], 1e-16, None, ALU.add))
                c.last()
                c.done(nc.vector.reciprocal(den[:, :, :], den[:, :, :]))
                c.last()
                a4 = agg[:, :, :].rearrange("p t (h c) -> p t h c", c=NE)
                c.done(nc.vector.tensor_tensor(a4, a4, den[:, :, :, None].broadcast_to([P, NT, HEADS, NE]), ALU.mult))
                dve.wait_ge(s_w, 48)
                c.last()

                def rowwise(x, y, op):
                    c.done(nc.vector.tensor_tensor(x[:, :, :], x[:, :, :], y, op))
                    c.last()

                rowwise(agg, bgat[:, None, :].broadcast_to([P, NT, HC]), ALU.add)
                c.done(nc.vector.tensor_reduce(v[:, :], agg[:, :, :], AX.X, ALU.add))
                c.last()
                c.done(nc.vector.tensor_scalar(v[:, :], v[:, :], 1.0 / HC, None, ALU.mult))
                c.last()
                rowwise(agg, v[:, :, None].broadcast_to([P, NT, HC]), ALU.subtract)
                c.done(nc.vector.tensor_tensor(a1[:, :, :], agg[:, :, :], agg[:, :, :], ALU.mult))
                c.last()
                c.done(nc.vector.tensor_reduce(v[:, :], a1[:, :, :], AX.X, ALU.add))
                c.last()
                c.done(nc.vector.tensor_scalar(v[:, :], v[:, :], 1.0 / HC, None, ALU.mult))
                c.last()
                rsqrt(nc, c, r[:, :], v[:, :], t1[:, :], ri[:, :], s_d)
                c.n += 1
                c.last()
                rowwise(agg, r[:, :, None].broadcast_to([P, NT, HC]), ALU.mult)
                rowwise(agg, fg[:, None, :].broadcast_to([P, NT, HC]), ALU.mult)
                rowwise(agg, fb[:, None, :].broadcast_to([P, NT, HC]), ALU.add)
                c.done(nc.vector.tensor_reduce(sc[:, :, :], agg[:, :, :].rearrange("p t (h c) -> p t c h", c=NE), AX.X, ALU.add))
                c.last()
                c.done(nc.vector.tensor_scalar(sc[:, :, :], sc[:, :, :], 1.0 / HEADS, None, ALU.mult))
                c.last()
                col = sc[:, :, None, :].broadcast_to([P, NT, NE, NE])
                rowe = sc[:, :, :, None].broadcast_to([P, NT, NE, NE])
                c.done(nc.vector.tensor_tensor(wins[:, :, :, :], col, rowe, ALU.is_gt))
                c.done(nc.vector.tensor_tensor(ties[:, :, :, :], col, rowe, ALU.is_equal))
                c.done(nc.vector.tensor_reduce(v[:, :], sc[:, :, :], AX.X, ALU.max))
                c.last()
                c.done(nc.vector.tensor_tensor(ties[:, :, :, :], ties[:, :, :, :], low[:, None, :, :].broadcast_to([P, NT, NE, NE]), ALU.mult))
                nc.vector.tensor_tensor(g[:, :, :], sc[:, :, :], v[:, :, None].broadcast_to([P, NT, NE]), ALU.subtract).then_inc(s_gs, 1)
                c.last()
                c.done(nc.vector.tensor_tensor(wins[:, :, :, :], wins[:, :, :, :], ties[:, :, :, :], ALU.add))
                c.last()
                c.done(nc.vector.tensor_reduce(sel[:, :, :], wins[:, :, :, :], AX.X, ALU.add))
                c.last()
                c.done(nc.vector.tensor_scalar(sel[:, :, :], sel[:, :, :], 1.5, None, ALU.is_lt))
                c.last()
                dve.wait_ge(s_ge, 1)
                rowwise(g, sel[:, :, :], ALU.mult)
                c.done(nc.vector.tensor_reduce(v[:, :], g[:, :, :], AX.X, ALU.add))
                c.last()
                c.done(nc.vector.reciprocal(r[:, :], v[:, :]))
                c.last()
                rowwise(g, r[:, :, None].broadcast_to([P, NT, NE]), ALU.mult)

                def combine(j, b, T):
                    i = j * 2 + b
                    s = Steps(dve, s_dc, i, (NE - 1) * G + G - 1)
                    dve.wait_ge(s_eo[b], j * (16 * NE) + 16 * NE)
                    dve.wait_ge(s_st[b], j * 16)
                    for x in range(NE):
                        for t in range(T):
                            n = i * G + t
                            before = acc[:, b, t, :] if x else M["xn"][:, n, :]
                            y = nc.vector.scalar_tensor_tensor(acc[:, b, t, :], eo[:, b, x, t, :], g[:, n, x:x + 1], before, ALU.mult, ALU.add)
                            if x < NE - 1 or t < T - 1:
                                s.done(y)
                        if x < NE - 1:
                            s.last()
                    y.then_inc(s_out, 1)
                    s.end(T == G)

                over_groups(dve, combine)


def layout(inputs):
    import numpy as np
    t = lambda a: np.ascontiguousarray(np.asarray(a))
    col = lambda a: np.ascontiguousarray(np.asarray(a).reshape(-1, P).T)
    g, m, f = "L0_gnn_", "L0_mix_", "L0_ffn_"
    return {
        "x": t(inputs["x"]), "src": t(inputs["src"]), "dst": t(inputs["dst"]), "ea": t(inputs["edge_attr_64"]),
        "We": t(inputs[g + "We"]), "be": t(inputs[g + "be"]), "gW1": t(inputs[g + "W1"]), "gb1": col(inputs[g + "b1"]),
        "gW2": t(inputs[g + "W2"]), "gb2": t(inputs[g + "b2"]), "gg": t(inputs[g + "gamma"]), "gb": t(inputs[g + "beta"]),
        "l1w": col(inputs[m + "ln1_w"]), "l1b": col(inputs[m + "ln1_b"]), "l2w": col(inputs[m + "ln2_w"]), "l2b": col(inputs[m + "ln2_b"]),
        "WxT": t(np.asarray(inputs[m + "Wx"]).T), "bx": col(inputs[m + "bx"]), "WqT": t(np.asarray(inputs[m + "Wq"]).T),
        "WkT": t(np.asarray(inputs[m + "Wk"]).T), "WvT": t(np.asarray(inputs[m + "Wv"]).T),
        "WoT": t(np.asarray(inputs[m + "Wo"]).T), "bo": t(inputs[m + "bo"]),
        "mW1T": t(np.asarray(inputs[m + "W1"]).T), "mb1": col(inputs[m + "b1"]), "mW2T": t(np.asarray(inputs[m + "W2"]).T), "mb2": t(inputs[m + "b2"]),
        "Wgat": t(inputs[f + "W_gat"]), "asrc": t(inputs[f + "att_src"]), "adst": t(inputs[f + "att_dst"]), "bgat": t(inputs[f + "b_gat"]),
        "fg": t(inputs[f + "ln_gamma"]), "fb": t(inputs[f + "ln_beta"]), "eW1": t(inputs[f + "W1"]), "eb1": col(inputs[f + "b1"]),
        "eW2": t(inputs[f + "W2"]), "eb2": t(inputs[f + "b2"]), "ei": t(inputs[f + "edge_index"]),
    }


def kernel(**inputs):
    import concourse.bacc as bacc
    from concourse import mybir as mb
    from concourse.bass_utils import run_bass_kernel_spmd

    nc = bacc.Bacc("TRN2", target_bir_lowering=False, num_devices=1)
    arrays = {"in_" + k: v for k, v in layout(inputs).items()}
    A = {k[3:]: nc.dram_tensor(k, v.shape, mb.dt.from_np(v.dtype), kind="ExternalInput").ap() for k, v in arrays.items()}
    out = nc.dram_tensor("out", (N, D), mb.dt.float32, kind="ExternalOutput").ap()
    build(nc, A, out)
    r = run_bass_kernel_spmd(nc, [arrays], core_ids=[0])
    return r.results[0]["out"]
```
